# Optimizing a Trainium2 kernel written in Bass

```python
import numpy as np
import jax
import jax.numpy as jnp

def _softmax(x, axis=-1):
    return jax.nn.softmax(x, axis=axis)

def _gelu(x):
    return jax.nn.gelu(x, approximate=True)

def _silu(x):
    return jax.nn.silu(x)

def _sigmoid(x):
    return jax.nn.sigmoid(x)

def _layernorm(x, axis=-1, eps=1e-05):
    m = jnp.mean(x, axis=axis, keepdims=True)
    v = jnp.var(x, axis=axis, keepdims=True)
    return (x - m) / jnp.sqrt(v + eps)

def _scatter_add(tgt, idx, src, axis=0):
    return tgt.at[idx].add(src)

def _segment_sum(src, seg, n):
    return jax.ops.segment_sum(src, seg, n)
kernel_name = 'mk_macaron_d1_jaxref_r8_a09fb3'

def setup_inputs(seed: int=0):
    np.random.seed(seed)
    _w = jnp.asarray

    def _L0_attn_setup():
        import jax, jax.numpy as jnp
        import numpy as np
        HIDDEN = 256
        HEADS = 16
        HEAD_DIM = HIDDEN // HEADS
        NEG = -10000000000.0
        key = jax.random.key(seed)
        k1, k2, k3 = jax.random.split(key, 3)
        x = jax.random.normal(k1, (2, 256, HIDDEN), dtype=jnp.float32)
        w_qkv = jax.random.normal(k2, (HIDDEN, 3 * HIDDEN), dtype=jnp.float32) / np.sqrt(HIDDEN)
        w_out = jax.random.normal(k3, (HIDDEN, HIDDEN), dtype=jnp.float32) / np.sqrt(HIDDEN)
        return {'x': x, 'w_qkv': w_qkv, 'w_out': w_out}
    _L0_attn_in = _L0_attn_setup()

    def _L0_ffn_setup():
        import jax, jax.numpy as jnp
        import numpy as np
        B, S, H, E, I, TOPK = (1, 128, 256, 16, 128, 2)
        SCALE = 1.0
        key = jax.random.key(seed)
        k0, k1, k2, k3 = jax.random.split(key, 4)
        hidden_states = jax.random.normal(k0, (B, S, H), dtype=jnp.float32)
        gate_w = jax.random.normal(k1, (E, H), dtype=jnp.float32) * 0.02
        gate_up_proj = jax.random.normal(k2, (E, H, 2 * I), dtype=jnp.float32) / np.sqrt(H)
        down_proj = jax.random.normal(k3, (E, I, H), dtype=jnp.float32) / np.sqrt(I)
        return {'hidden_states': hidden_states, 'gate_w': gate_w, 'gate_up_proj': gate_up_proj, 'down_proj': down_proj}
    _L0_ffn_in = _L0_ffn_setup()
    _d = {'L0_attn_x': _L0_attn_in['x'], 'L0_attn_w_qkv': _L0_attn_in['w_qkv'], 'L0_attn_w_out': _L0_attn_in['w_out'], 'L0_ffn_gate_w': _L0_ffn_in['gate_w'], 'L0_ffn_gate_up_proj': _L0_ffn_in['gate_up_proj'], 'L0_ffn_down_proj': _L0_ffn_in['down_proj']}
    _x0 = _d['L0_attn_x']
    _d['L0_attn_x'] = jax.random.normal(jax.random.fold_in(jax.random.key(seed), 1), (16, 256, 256), dtype=_x0.dtype)
    del _x0
    return _d

def reference(L0_attn_x, L0_attn_w_qkv, L0_attn_w_out, L0_ffn_gate_w, L0_ffn_gate_up_proj, L0_ffn_down_proj):

    def _L0_attn_ref(x, w_qkv, w_out):
        import jax, jax.numpy as jnp
        import numpy as np
        HIDDEN = 256
        HEADS = 16
        HEAD_DIM = HIDDEN // HEADS
        NEG = -10000000000.0
        b, s, _ = x.shape
        qkv = x @ w_qkv
        qkv = qkv.reshape(b, s, 3, HEADS, HEAD_DIM)
        q, k, v = (qkv[:, :, 0], qkv[:, :, 1], qkv[:, :, 2])
        scale = jnp.sqrt(jnp.float32(HEAD_DIM)).astype(x.dtype)
        q = q / scale
        scores = jnp.einsum('bqhd,bkhd->bhqk', q, k)
        causal_mask = jnp.arange(s)[:, None] >= jnp.arange(s)[None, :]
        scores = jnp.where(causal_mask[None, None], scores, NEG)
        attn = jax.nn.softmax(scores, axis=-1)
        out = jnp.einsum('bhqk,bkhd->bqhd', attn, v).reshape(b, s, HIDDEN)
        return out @ w_out

    def _L0_ffn_ref(hidden_states, gate_w, gate_up_proj, down_proj):
        import jax, jax.numpy as jnp
        import numpy as np
        B, S, H, E, I, TOPK = (1, 128, 256, 16, 128, 2)
        SCALE = 1.0
        b, s, h = hidden_states.shape
        e = gate_w.shape[0]
        x = hidden_states.reshape(-1, h)
        logits = jnp.matmul(x.astype(jnp.float32), gate_w.T.astype(jnp.float32))
        p = jax.nn.sigmoid(logits)
        p = p / jnp.sum(p, axis=-1, keepdims=True)
        w, idx = jax.lax.top_k(p, TOPK)
        w = w / jnp.sum(w, axis=-1, keepdims=True)
        w = w * SCALE
        combine = jnp.sum(jax.nn.one_hot(idx, e, dtype=w.dtype) * w[..., None], axis=1)
        gu = jnp.einsum('th,ehf->etf', x, gate_up_proj)
        gate, up = jnp.split(gu, 2, axis=-1)
        inter = jax.nn.silu(gate) * up
        y = jnp.einsum('eti,eih->eth', inter, down_proj)
        out = jnp.einsum('eth,te->th', y, combine.astype(y.dtype))
        return out.reshape(b, s, h)
    x = L0_attn_x
    x = x + 0.5 * _L0_ffn_ref(_layernorm(x, axis=-1), L0_ffn_gate_w, L0_ffn_gate_up_proj, L0_ffn_down_proj)
    x = x + _L0_attn_ref(_layernorm(x, axis=-1), L0_attn_w_qkv, L0_attn_w_out)
    x = x + 0.5 * _L0_ffn_ref(_layernorm(x, axis=-1), L0_ffn_gate_w, L0_ffn_gate_up_proj, L0_ffn_down_proj)
    return x

_drawn_inputs = setup_inputs


def setup_inputs(seed=0):
    import zlib

    import numpy as np

    out = dict(_drawn_inputs(seed))
    spreads = {}
    factors = {}
    for name, (base, spread) in spreads.items():
        noise = np.random.default_rng([zlib.crc32(name.encode()), seed]).standard_normal(out[name].shape)
        drawn = base * np.exp(spread * noise) if base else spread * noise
        out[name] = jnp.asarray(drawn.astype(out[name].dtype))
    for name, factor in factors.items():
        out[name] = (out[name] * factor).astype(out[name].dtype)
    return out
```

```python
import concourse.bass as bass
from concourse import mybir
from contextlib import ExitStack

F32 = mybir.dt.float32
BF16 = mybir.dt.bfloat16
U32 = mybir.dt.uint32
I32 = mybir.dt.int32
ALU = mybir.AluOpType
ACT = mybir.ActivationFunctionType
AX = mybir.AxisListType

P = 128


def macaron_block(nc, x_in, w_qkv, w_out, gate_w, gate_up, down, out, stages=("ffn", "attn", "ffn")):
    B, S, H = x_in.shape
    NT = B * S // P
    HC = H // P
    E = gate_w.shape[0]
    I = down.shape[1]
    TOPK = 2
    NE_T = B * S * TOPK // P + E
    RING = 4
    NK = NE_T // RING
    LOADS = 4
    EPS = 1e-5
    HEADS, D = 16, H // 16
    NEG = -1e30
    SLOTS = 7
    VW = 32
    G = HEADS // 4
    NF = stages.count("ffn")

    x_tiles = x_in.rearrange("b (n p) h -> p (b n) h", p=P)
    out_tiles = out.rearrange("b (n p) h -> p (b n) h", p=P)

    grouped_in = nc.dram_tensor("grouped_in", [NE_T * P, H], F32).ap()
    grouped_out = nc.dram_tensor("grouped_out", [NE_T * P, H], F32).ap()

    ctx = ExitStack()
    with ctx:
        def sb(name, shape, dt=F32):
            return ctx.enter_context(nc.sbuf_tensor(name, shape, dt))

        def sem(name):
            return ctx.enter_context(nc.semaphore(name))

        bank = [ctx.enter_context(nc.psum_tensor(f"bank{i}", [P, 512], F32)) for i in range(8)]

        shared = sb("shared", [P, 4 * HEADS * S // 2])
        taken = [0]

        def lay(n, dims, **sizes):
            taken[0] += n
            assert taken[0] <= 4 * HEADS * S // 2
            return shared[:, taken[0] - n:taken[0]].rearrange(dims, **sizes)

        x_sb = sb("x_sb", [P, NT, H])
        wgu_sb = sb("wgu_sb", [P, E, HC, 2 * I])
        wd_sb = sb("wd_sb", [P, E, H])
        gw_sb = sb("gw_sb", [E, H])
        gwT = sb("gwT", [P, HC, E])
        ident = sb("ident", [P, P])
        tri = sb("tri", [P, P], BF16)
        ones = sb("ones", [P, P], BF16)
        rev = sb("rev", [P, E])
        thr = sb("thr", [P, NT])
        tile_no = sb("tile_no", [1, NE_T])
        one_e = sb("one_e", [P, E])
        seg = sb("seg", [P, E, NT])
        stats = sb("stats", [P, NT, 6])
        msum = sb("msum", [P, NT])
        mdif = sb("mdif", [P, NT])
        vsum = sb("vsum", [P, NT])
        mean = sb("mean", [P, NT])
        var = sb("var", [P, NT])
        std = sb("std", [P, NT])
        rstd = sb("rstd", [P, NT])
        xn = sb("xn", [P, 2, H])
        xnT = sb("xnT", [P, 2, HC, P])
        prob = lay(NT * E, "p (t e) -> p t e", e=E)
        top = [sb(f"top{k}", [P, NT]) for k in range(TOPK)]
        eq = lay(NT * E, "p (t e) -> p t e", e=E)
        cand = lay(NT * E, "p (t e) -> p t e", e=E)
        first = sb("first", [P, NT])
        pick = [lay(NT * E, "p (t e) -> p t e", e=E) for k in range(TOPK)]
        rest = lay(NT * E, "p (t e) -> p t e", e=E)
        picks = sb("picks", [P, NT, E], BF16)
        wsum = sb("wsum", [P, NT])
        wrec = sb("wrec", [P, NT])
        weight = sb("weight", [P, NT, TOPK])
        tot = lay(E * NT, "p (e t) -> p e t", e=E)
        cum = lay(E * NT, "p (e t) -> p e t", e=E)
        more = lay(E * NT, "p (e t) -> p e t", e=E)
        ntile = sb("ntile", [P, E])
        end = sb("end", [P, E])
        begin = sb("begin", [P, E])
        slot_e = more
        slot_t = lay(NT * E, "p (t e) -> p t e", e=E)
        slot_f = sb("slot_f", [P, NT, TOPK])
        slot = sb("slot", [P, NT, TOPK], U32)
        past = sb("past", [1, NE_T, E])
        eid_f = sb("eid_f", [1, NE_T])
        eid = sb("eid", [1, NE_T], I32)
        wqkv_sb = sb("wqkv_sb", [P, HC, 3 * H])
        wout_sb = sb("wout_sb", [P, HC, H])
        ident_b = sb("ident_b", [P, P], BF16)
        future = sb("future", [P, 4, P], BF16)
        head_sel = sb("head_sel", [P, HEADS, P], BF16)
        an = sb("an", [P, 2, H])
        anT = sb("anT", [P, HC, S])
        stack = [sb(f"stack{u}", [P, 2, HEADS, SLOTS, D], BF16) for u in range(2)]
        left = [sb(f"left{u}", [P, 2, HEADS, D]) for u in range(2)]
        half = HEADS * S // 2
        qT, kT = ([shared[0:SLOTS * D, (2 * a + i) * half:(2 * a + i + 1) * half].bitcast(BF16)
                   .rearrange("p (h n) -> p h n", h=HEADS) for i in range(2)] for a in range(2))
        v_sb = [sb(f"v_sb{i}", [P, 2, HEADS, VW]) for i in range(2)]
        mx = sb("mx", [P, 2, HEADS])
        nleft = sb("nleft", [P, 2, HEADS])
        nmax = sb("nmax", [P, 2, P], BF16)
        nmaxT = [sb(f"nmaxT{i}", [P, S], BF16) for i in range(2)]
        pr0 = [sb(f"pr0_{i}", [P, 4, S]) for i in range(2)]
        pr1 = [sb(f"pr1_{i}", [P, 4, P]) for i in range(2)]
        oT = sb("oT", [P, HEADS // 4, S])
        rsum = sb("rsum", [P, HEADS])
        att = sb("att", [P, H])
        attT = sb("attT", [P, HC, P])
        idx = [[sb(f"idx{r}_{k}", [P, 1], U32) for k in range(TOPK)] for r in range(RING)]
        gathered_rows = lay(RING * TOPK * H, "p (r k h) -> p r k h", r=RING, k=TOPK)
        got = [[gathered_rows[:, r, k, :] for k in range(TOPK)] for r in range(RING)]
        zeros = gathered_rows.rearrange("p r k h -> p (r k h)")
        xe = lay(RING * H, "p (r h) -> p r h", r=RING)
        row_out = [xe[:, r, :] for r in range(RING)]
        xeT = sb("xeT", [P, 2, HC, P])
        silu = sb("silu", [P, 2, I])
        hid = sb("hid", [P, 2, I])
        hidT = sb("hidT", [P, 2, P])
        ye = sb("ye", [P, RING, H])
        mix = sb("mix", [P, H])

        x_loaded = [sem(f"x_loaded{c}") for c in range(LOADS)]
        gw_loaded = sem("gw_loaded")
        wgu_loaded = sem("wgu_loaded")
        wd_loaded = sem("wd_loaded")
        zero_set = sem("zero_set")
        zero_filled = sem("zero_filled")
        consts = sem("consts")
        const_step = sem("const_step")
        gwT_made = sem("gwT_made")
        gwT_ready = sem("gwT_ready")
        all_stats = sem("all_stats")
        step = sem("step")
        stored = sem("stored")
        pool_turn = sem("pool_turn")

        def ffn_sems(f):
            names = ("stats_done", "var_ready", "std_ready", "rstd_ready", "xn_ready", "xn_transposed", "xnT_ready",
                     "logits_done", "prob_ready", "picks_ready", "counts_done", "eid_ready", "rows_ready",
                     "xe_transposed", "xeT_ready", "gu_done", "silu_ready", "hid_ready", "hid_transposed",
                     "hidT_ready", "down_done", "ye_ready", "idx_ready", "mix_ready", "x_done")
            rings = ("scattered", "xe_loaded", "ye_stored", "gathered")
            found = {n: sem(f"{n}_f{f}") for n in names}
            found.update({n: [sem(f"{n}{r}_f{f}") for r in range(RING)] for n in rings})
            return found

        at = {n: sem(f"{n}_at") for n in (
            "var_ready", "std_ready", "rstd_ready", "an_ready", "an_transposed", "anT_ready", "qk_done", "hi_ready",
            "left_ready", "mid_ready", "low_ready", "parts_copied", "highs_copied", "v_done", "v_ready",
            "fill_done", "fill_act", "fill_dve", "score_done", "max_ready", "nmax_step", "nmax_ready", "nmax_transposed",
            "nmaxT_ready", "scoreT_done", "exp_ready", "masked", "pv_done", "oT_ready", "o_transposed",
            "rsum_ready", "att_ready", "att_transposed", "attT_ready", "proj_done", "x_done")}
        wqkv_loaded = sem("wqkv_loaded")
        wqkv_scaled = sem("wqkv_scaled")
        wout_loaded = sem("wout_loaded")
        att_consts = sem("att_consts")
        ffn = [ffn_sems(f) for f in range(NF)]
        count, waited = [0], [0]

        def link(dve, ins):
            count[0] += 1
            ins.then_inc(step, 1)
            dve.wait_ge(step, count[0])

        block = ctx.enter_context(nc.Block())

        FRONT = [("f", n) for n in ("norm", "qk0", "qk1", "v")] + [("fill", i) for i in range(8)] \
            + [("score", i) for i in range(3 * G)] + [("f", "max")]
        BACK = []
        for g in range(G):
            BACK += [("scoreT", 3 * g + i) for i in range(3)]
            if g:
                BACK += [("pv", g - 1)]
        BACK += [("pv", G - 1)] + [(n, u) for u in range(2) for n in ("untranspose", "transpose", "project")]

        def both():
            order, n = [], max(len(FRONT), len(BACK))
            for i in range(n):
                order += [(0, st) for st in FRONT[i * len(FRONT) // n:(i + 1) * len(FRONT) // n]]
                order += [(1, st) for st in BACK[i * len(BACK) // n:(i + 1) * len(BACK) // n]]
            return order

        BOTH = both()

        def batches(eng, part):
            for st in FRONT:
                part(st, 0, 0)
            for back, st in BOTH:
                part(st, 1 - back, 1 - back)
            with eng.Fori(1, B // 2) as m:
                for i in range(2):
                    for back, st in BOTH:
                        part(st, m * 2 + (i - back), (i - back) % 2)
            for st in BACK:
                part(st, B - 1, (B - 1) % 2)

        def later(eng, s, b, per, n):
            if isinstance(b, int) and per * b + n <= 0:
                return
            eng.wait_ge(s, b * per + n)

        bankA, bankB, bankC = bank[5], bank[6], bank[7]

        def fill_of(i):
            return i // 4, i // 2 % 2, i % 2 * 8, (bankA, bankB)[i % 2]

        def score_of(n):
            return (0, 4 * n, 4) if n < G else (1, 2 * (n - G), 2)

        def scoreT_of(n):
            g, i = n // 3, n % 3
            return (0, 4 * g + 2 * i, 2) if i < 2 else (1, 4 * g, 4)

        def attn_pool(pool):
            def part(st, b, p):
                kind, n = st
                if kind in ("f",) and n in ("qk0", "qk1"):
                    u = int(n[2])
                    later(pool, at["hi_ready"], b, 2, u + 1)
                    pool.sem_inc(pool_turn, 1)
                    for qk, to in ((0, 3), (1, 5)):
                        last = nc.gpsimd.tensor_copy(stack[u][:, qk, :, to:to + 2, :],
                                                     stack[u][:, qk, :, 0:1, :].broadcast_to([P, HEADS, 2, D]))
                    last.then_inc(at["highs_copied"], 1)
                if kind == "scoreT" and n % 3:
                    g, second = n // 3, n % 3 == 2
                    later(pool, at["exp_ready"], b, 3 * G, n + 1)
                    pool.sem_inc(pool_turn, 1)
                    m = (pr1 if second else pr0)[g % 2][:, :, 0:P]
                    nc.gpsimd.affine_select(out=m, in_=m, compare_op=ALU.is_ge, fill=0.0, base=0,
                                            pattern=[[0, 4], [1, P]], channel_multiplier=-1).then_inc(at["masked"], 1)
            batches(pool, part)

        def attn_tensor(pe):
            pe.wait_ge(wqkv_scaled, 1)
            pe.wait_ge(wout_loaded, 16)
            pe.wait_ge(att_consts, 5)

            def qk_product(u, b, dst):
                for c in range(HC):
                    last = nc.tensor.matmul(dst[:, :], anT[:, c, u * P:(u + 1) * P], wqkv_sb[:, c, 0:2 * H],
                                            start=(c == 0), stop=(c == HC - 1))
                last.then_inc(at["qk_done"], 1)

            def part(st, b, p):
                kind, n = st
                if st == ("f", "norm"):
                    later(pe, at["an_ready"], b, 2, 2)
                    later(pe, at["nmaxT_ready"], b, 1, 0)
                    for u in range(2):
                        for c in range(HC):
                            last = nc.tensor.transpose(bankA[:, c * S + u * P:c * S + (u + 1) * P],
                                                       an[:, u, c * P:(c + 1) * P], ident[:, :])
                    last.then_inc(at["an_transposed"], 1)
                elif st == ("f", "qk0"):
                    later(pe, at["anT_ready"], b, 1, 1)
                    later(pe, at["fill_dve"], b, 4, 0)
                    qk_product(0, b, bankB)
                elif st == ("f", "qk1"):
                    qk_product(1, b, bankA)
                elif st == ("f", "v"):
                    later(pe, at["left_ready"], b, 2, 1)
                    for u in range(2):
                        for c in range(HC):
                            last = nc.tensor.matmul(bankB[:, u * H:(u + 1) * H], anT[:, c, u * P:(u + 1) * P],
                                                    wqkv_sb[:, c, 2 * H:3 * H], start=(c == 0), stop=(c == HC - 1))
                    last.then_inc(at["v_done"], 1)
                elif kind == "fill":
                    u, qk, h0, dst = fill_of(n)
                    later(pe, at["parts_copied"], b, 2, u + 1)
                    later(pe, at["highs_copied"], b, 2, u + 1)
                    if n == 0:
                        later(pe, at["left_ready"], b, 2, 2)
                    elif n == 1:
                        later(pe, at["v_ready"], b, 1, 1)
                    else:
                        later(pe, (at["fill_act"], at["fill_dve"])[n % 2], b, 4, n // 2)
                    for i in range(8):
                        last = nc.tensor.transpose(dst[:, :].bitcast(BF16)[0:SLOTS * D, i * P:(i + 1) * P],
                                                   stack[u][:, qk, h0 + i, :, :].rearrange("p s d -> p (s d)"), ident_b[:, :])
                    last.then_inc(at["fill_done"], 1)
                elif kind == "score":
                    u, h0, nh = score_of(n)
                    later(pe, at["fill_act"], b, 4, 2 * (u + 1))
                    later(pe, at["fill_dve"], b, 4, 2 * (u + 1))
                    later(pe, at["max_ready"], b, 3 * G, n - 1)
                    dst, w = bank[3 + n % 2], P * (u + 1)
                    for i in range(nh):
                        nc.tensor.matmul(dst[:, i * w:(i + 1) * w], qT[p][:, h0 + i, u * P:(u + 1) * P], kT[p][:, h0 + i, 0:w],
                                         start=(i == 0), stop=False, skip_group_check=True)
                    diag = dst[:, :].rearrange("p (h k) -> p h k", k=w)[:, :, u * P:(u + 1) * P]
                    nc.tensor.matmul(diag, ident_b[:, :], future[:, 0:nh, :], start=False, stop=True,
                                     skip_group_check=True).then_inc(at["score_done"], 1)
                elif st == ("f", "max"):
                    later(pe, at["nmax_ready"], b, 1, 1)
                    later(pe, at["fill_act"], b, 4, 4)
                    for u in range(2):
                        last = nc.tensor.transpose(bankA[:, :].bitcast(BF16)[:, u * P:(u + 1) * P], nmax[:, u, :], ident_b[:, :])
                    last.then_inc(at["nmax_transposed"], 1)
                elif kind == "scoreT":
                    kt, h0, nh = scoreT_of(n)
                    later(pe, at["nmaxT_ready"], b, 1, 1)
                    later(pe, at["exp_ready"], b, 3 * G, n - 2)
                    dst, w = bank[n % 3], S - kt * P
                    for i in range(nh):
                        h = h0 + i
                        nc.tensor.matmul(dst[:, i * w:(i + 1) * w], kT[p][:, h, kt * P:(kt + 1) * P], qT[p][:, h, kt * P:S],
                                         start=(i == 0), stop=False, skip_group_check=True)
                        last = nc.tensor.matmul(dst[:, i * w:(i + 1) * w], head_sel[:, h, :], nmaxT[p][:, kt * P:S],
                                                start=False, stop=True, skip_group_check=True)
                    last.then_inc(at["scoreT_done"], 1)
                elif kind == "pv":
                    later(pe, at["masked"], b, 2 * G, 2 * n + 2)
                    later(pe, at["oT_ready"], b, G, n)
                    if n == 0:
                        later(pe, at["x_done"], b, 2, 0)
                    cols = n % 2 * S
                    for kt in range(2):
                        for j in range(4):
                            rhs = pr0[n % 2][:, j, :] if kt == 0 else pr1[n % 2][:, j, :]
                            last = nc.tensor.matmul(bankC[j * VW:(j + 1) * VW, cols + kt * P:cols + S],
                                                    v_sb[p][:, kt, 4 * n + j, :], rhs, start=(kt == 0), stop=(kt == 1),
                                                    skip_group_check=True)
                    last.then_inc(at["pv_done"], 1)
                elif kind == "untranspose":
                    later(pe, at["oT_ready"], b, G, G)
                    if n:
                        later(pe, at["x_done"], b, 2, 1)
                    for g in range(G):
                        last = nc.tensor.transpose(bankC[:, g * P:(g + 1) * P], oT[:, g, n * P:(n + 1) * P], ident[:, :])
                    last.then_inc(at["o_transposed"], 1)
                elif kind == "transpose":
                    later(pe, at["att_ready"], b, 2, n + 1)
                    for c in range(HC):
                        last = nc.tensor.transpose(bankC[:, c * P:(c + 1) * P], att[:, c * P:(c + 1) * P], ident[:, :])
                    last.then_inc(at["att_transposed"], 1)
                elif kind == "project":
                    later(pe, at["attT_ready"], b, 2, n + 1)
                    for c in range(HC):
                        last = nc.tensor.matmul(bankC[:, 0:H], attT[:, c, :], wout_sb[:, c, :], start=(c == 0), stop=(c == HC - 1))
                    last.then_inc(at["proj_done"], 1)
            batches(pe, part)

        def attn_scalar(act):
            act.wait_ge(at["var_ready"], 1)
            nc.scalar.activation(std[:, :], var[:, :], ACT.Sqrt).then_inc(at["std_ready"], 1)

            def part(st, b, p):
                kind, n = st
                if st == ("f", "norm"):
                    later(act, at["an_transposed"], b, 1, 1)
                    nc.scalar.activation(anT[:, :, :].rearrange("p c n -> p (c n)"), bankA[:, :], ACT.Copy).then_inc(at["anT_ready"], 1)
                elif kind == "f" and n in ("qk0", "qk1"):
                    u = int(n[2])
                    src = (bankB, bankA)[u]
                    later(act, at["qk_done"], b, 2, u + 1)
                    nc.scalar.activation(stack[u][:, :, :, 0, :].rearrange("p a h d -> p (a h) d"),
                                         src[:, :].rearrange("p (h d) -> p h d", d=D), ACT.Copy).then_inc(at["hi_ready"], 1)
                    later(act, at["left_ready"], b, 2, u + 1)
                    nc.scalar.activation(stack[u][:, :, :, 1, :].rearrange("p a h d -> p (a h) d"),
                                         left[u][:, :, :, :].rearrange("p a h d -> p (a h) d"), ACT.Copy).then_inc(at["mid_ready"], 1)
                elif kind == "fill" and n % 2 == 0:
                    u, qk, h0, src = fill_of(n)
                    later(act, at["fill_done"], b, 8, n + 1)
                    dst = (qT, kT)[qk][p]
                    nc.scalar.activation(dst[:, h0:h0 + 8, u * P:(u + 1) * P],
                                         src[:, :].bitcast(BF16)[0:SLOTS * D, :].rearrange("p (h n) -> p h n", n=P),
                                         ACT.Copy).then_inc(at["fill_act"], 1)
                elif st == ("f", "max"):
                    later(act, at["nmax_transposed"], b, 1, 1)
                    nc.scalar.activation(nmaxT[p][:, :], bankA[:, :].bitcast(BF16)[:, 0:S], ACT.Copy).then_inc(at["nmaxT_ready"], 1)
                elif kind == "scoreT":
                    kt, h0, nh = scoreT_of(n)
                    g = n // 3
                    later(act, at["scoreT_done"], b, 3 * G, n + 1)
                    if n % 3 == 0:
                        later(act, at["pv_done"], b, G, g - 1)
                    dst = pr1[g % 2][:, :, :] if kt else pr0[g % 2][:, h0 % 4:h0 % 4 + 2, :]
                    nc.scalar.activation(dst.rearrange("p h n -> p (h n)"), bank[n % 3][:, :], ACT.Exp).then_inc(at["exp_ready"], 1)
                elif kind == "transpose":
                    later(act, at["att_transposed"], b, 2, n + 1)
                    nc.scalar.activation(attT[:, :, :].rearrange("p c n -> p (c n)"), bankC[:, 0:H], ACT.Copy).then_inc(at["attT_ready"], 1)
            batches(act, part)

        def attn_vector(dve):
            layernorm_scale(dve, at)

            def split(u, b):
                src = (bankB, bankA)[u]
                later(dve, at["hi_ready"], b, 2, u + 1)
                nc.vector.tensor_tensor(left[u][:, :, :, :].rearrange("p a h d -> p (a h) d"),
                                        src[:, :].rearrange("p (h d) -> p h d", d=D),
                                        stack[u][:, :, :, 0, :].rearrange("p a h d -> p (a h) d"), ALU.subtract)\
                    .then_inc(at["left_ready"], 1)

            def split_low(u, b):
                later(dve, at["mid_ready"], b, 2, u + 1)
                nc.vector.tensor_tensor(stack[u][:, :, :, 2, :].rearrange("p a h d -> p (a h) d"),
                                        left[u][:, :, :, :].rearrange("p a h d -> p (a h) d"),
                                        stack[u][:, :, :, 1, :].rearrange("p a h d -> p (a h) d"), ALU.subtract)\
                    .then_inc(at["low_ready"], 1)
                later(dve, at["low_ready"], b, 2, u + 1)
                for qk, to in ((0, 5), (1, 3)):
                    last = nc.vector.tensor_copy(stack[u][:, qk, :, to:to + 2, :], stack[u][:, qk, :, 1:3, :])
                last.then_inc(at["parts_copied"], 1)

            def part(st, b, p):
                kind, n = st
                if st == ("f", "norm"):
                    later(dve, at["an_transposed"], b, 1, 0)
                    for u in range(2):
                        normalise(an[:, u, :], b * 2 + u).then_inc(at["an_ready"], 1)
                elif st == ("f", "qk0"):
                    split(0, b)
                elif st == ("f", "qk1"):
                    split(1, b)
                    split_low(0, b)
                elif st == ("f", "v"):
                    later(dve, at["v_done"], b, 1, 1)
                    nc.vector.tensor_copy(v_sb[p][:, :, :, 0:D], bankB[:, :].rearrange("p (u h d) -> p u h d", u=2, d=D))\
                        .then_inc(at["v_ready"], 1)
                    split_low(1, b)
                elif kind == "fill" and n % 2 == 1:
                    u, qk, h0, src = fill_of(n)
                    later(dve, at["fill_done"], b, 8, n + 1)
                    dst = (qT, kT)[qk][p]
                    nc.vector.tensor_copy(dst[:, h0:h0 + 8, u * P:(u + 1) * P],
                                          src[:, :].bitcast(BF16)[0:SLOTS * D, :].rearrange("p (h n) -> p h n", n=P))\
                        .then_inc(at["fill_dve"], 1)
                elif kind == "score":
                    u, h0, nh = score_of(n)
                    later(dve, at["score_done"], b, 3 * G, n + 1)
                    nc.vector.tensor_reduce(mx[:, u, h0:h0 + nh], bank[3 + n % 2][:, :].rearrange("p (h k) -> p h k", h=nh),
                                            AX.X, ALU.max).then_inc(at["max_ready"], 1)
                elif st == ("f", "max"):
                    later(dve, at["max_ready"], b, 3 * G, 3 * G)
                    nc.vector.tensor_scalar(nmax[:, :, 0:HEADS], mx[:, :, :], -1.0, None, ALU.mult).then_inc(at["nmax_step"], 1)
                    later(dve, at["nmax_step"], b, 3, 1)
                    nc.vector.scalar_tensor_tensor(out=nleft[:, :, :], in0=mx[:, :, :], scalar=-1.0, in1=nmax[:, :, 0:HEADS],
                                                   op0=ALU.mult, op1=ALU.subtract).then_inc(at["nmax_step"], 1)
                    later(dve, at["nmax_step"], b, 3, 2)
                    nc.vector.tensor_copy(nmax[:, :, HEADS:2 * HEADS], nleft[:, :, :]).then_inc(at["nmax_step"], 1)
                    later(dve, at["nmax_step"], b, 3, 3)
                    nc.vector.tensor_tensor(nmax[:, :, 2 * HEADS:3 * HEADS], nleft[:, :, :], nmax[:, :, HEADS:2 * HEADS],
                                            ALU.subtract).then_inc(at["nmax_ready"], 1)
                elif kind == "pv":
                    later(dve, at["pv_done"], b, G, n + 1)
                    nc.vector.tensor_copy(oT[:, n, :], bankC[:, n % 2 * S:(n % 2 + 1) * S]).then_inc(at["oT_ready"], 1)
                elif kind == "untranspose":
                    later(dve, at["o_transposed"], b, 2, n + 1)
                    o = bankC[:, :].rearrange("p (h d) -> p h d", d=VW)
                    nc.vector.reciprocal(rsum[:, :], o[:, :, D]).then_inc(at["rsum_ready"], 1)
                    later(dve, at["rsum_ready"], b, 2, n + 1)
                    nc.vector.tensor_tensor(att[:, :].rearrange("p (h d) -> p h d", d=D), o[:, :, 0:D],
                                            rsum[:, :].unsqueeze(2).broadcast_to([P, HEADS, D]), ALU.mult).then_inc(at["att_ready"], 1)
                elif kind == "project":
                    later(dve, at["proj_done"], b, 2, n + 1)
                    t = b * 2 + n
                    nc.vector.tensor_tensor(x_sb[:, t, :], bankC[:, 0:H], x_sb[:, t, :], ALU.add).then_inc(at["x_done"], 1)
                    later(dve, at["x_done"], b, 2, n + 1)
                    row_stats(t)
            batches(dve, part)

        def ffn_sync(sp, f):
            s = ffn[f]

            def load(r, k):
                sp.dma_start(xe[:, r, :], grouped_in[bass.ds((k * RING + r) * P, P), :]).then_inc(s["xe_loaded"][r], 16)

            def store(r, k):
                sp.wait_ge(s["ye_ready"], k * RING + r + 1)
                sp.dma_start(grouped_out[bass.ds((k * RING + r) * P, P), :], ye[:, r, :]).then_inc(s["ye_stored"][r], 16)

            for r in range(RING):
                sp.wait_ge(s["scattered"][r], 16 * TOPK * NT // RING)
            for r in range(RING):
                load(r, 0)
            with sp.Fori(0, NK - 1) as k:
                for r in range(RING):
                    store(r, k)
                    sp.wait_ge(s["xe_transposed"], k * RING + r + 1)
                    load(r, k + 1)
            for r in range(RING):
                store(r, NK - 1)

        @block.sync
        def _(sp):
            step_ = NT // LOADS
            for c in range(LOADS):
                sp.dma_start(x_sb[:, c * step_:(c + 1) * step_, :], x_tiles[:, c * step_:(c + 1) * step_, :]).then_inc(x_loaded[c], 16)
            for g in range(0, E, 4):
                if g == 4:
                    sp.dma_start(wqkv_sb[:, :, :], w_qkv.rearrange("(c p) f -> p c f", p=P)).then_inc(wqkv_loaded, 16)
                    sp.dma_start(wout_sb[:, :, :], w_out.rearrange("(c p) f -> p c f", p=P)).then_inc(wout_loaded, 16)
                for c in range(HC):
                    sp.dma_start(wgu_sb[:, g:g + 4, c, :],
                                 gate_up[g:g + 4, c * P:(c + 1) * P, :].rearrange("e p f -> p e f")).then_inc(wgu_loaded, 16)
                sp.dma_start(wd_sb[:, g:g + 4, :], down[g:g + 4].rearrange("e i h -> i e h")).then_inc(wd_loaded, 16)
            for n, st in enumerate(stages):
                if st == "ffn":
                    ffn_sync(sp, stages[:n].count("ffn"))
            s = ffn[NF - 1]
            with sp.Fori(0, NT // 2) as k:
                sp.wait_ge(s["x_done"], k * 2 + 2)
                sp.dma_start(out_tiles[:, bass.ds(k * 2, 2), :], x_sb[:, bass.ds(k * 2, 2), :]).then_inc(stored, 16)
            sp.wait_ge(stored, 16 * (NT // 2))

        def ffn_pool(pool, f):
            s = ffn[f]
            if f == 0:
                pool.wait_ge(zero_filled, 16 * (NE_T // 8))
            with pool.Fori(0, NT // RING) as k:
                for r in range(RING):
                    pool.wait_ge(s["rows_ready"], k * RING + r + 1)
                    pool.sem_inc(pool_turn, 1)
                    for j in range(TOPK):
                        nc.gpsimd.indirect_dma_start(grouped_in, bass.IndirectOffsetOnAxis(idx[r][j][:, :], 0),
                                                     row_out[r][:, :], None).then_inc(s["scattered"][r], 16)
            for r in range(RING):
                pool.wait_ge(s["ye_stored"][r], 16 * NK)
            with pool.Fori(0, NT // RING) as k:
                for r in range(RING):
                    pool.wait_ge(s["idx_ready"], k * RING + r + 1)
                    pool.sem_inc(pool_turn, 1)
                    for j in range(TOPK):
                        nc.gpsimd.indirect_dma_start(got[r][j], None, grouped_out,
                                                     bass.IndirectOffsetOnAxis(idx[r][j][:, :], 0)).then_inc(s["gathered"][r], 16)

        @block.gpsimd
        def _(pool):
            nc.gpsimd.memset(zeros[:, :], 0.0).then_inc(zero_set, 1)
            nc.gpsimd.memset(ident[:, :], 0.0).then_inc(const_step, 1)
            nc.gpsimd.memset(tri[:, :], 1.0).then_inc(const_step, 1)
            nc.gpsimd.memset(seg[:, :, :], 1.0).then_inc(const_step, 1)
            pool.wait_ge(const_step, 3)
            nc.gpsimd.affine_select(out=ident[:, :], in_=ident[:, :], compare_op=ALU.not_equal, fill=1.0,
                                    base=0, pattern=[[-1, P]], channel_multiplier=1).then_inc(consts, 1)
            nc.gpsimd.affine_select(out=tri[:, :], in_=tri[:, :], compare_op=ALU.is_gt, fill=0.0,
                                    base=0, pattern=[[1, P]], channel_multiplier=-1).then_inc(consts, 1)
            nc.gpsimd.memset(seg[:, :, 0:1], 0.0).then_inc(consts, 1)
            nc.gpsimd.memset(ones[:, :], 1.0).then_inc(consts, 1)
            nc.gpsimd.memset(one_e[:, :], 1.0).then_inc(consts, 1)
            nc.gpsimd.iota(rev[:, :], [[-1, E]], base=E, channel_multiplier=0,
                           allow_small_or_imprecise_dtypes=True).then_inc(consts, 1)
            nc.gpsimd.iota(thr[:, :], [[P, NT]], base=0, channel_multiplier=0,
                           allow_small_or_imprecise_dtypes=True).then_inc(consts, 1)
            nc.gpsimd.iota(tile_no[:, :], [[1, NE_T]], base=0, channel_multiplier=0,
                           allow_small_or_imprecise_dtypes=True).then_inc(consts, 1)
            nc.gpsimd.memset(ident_b[:, :], 0.0).then_inc(const_step, 1)
            nc.gpsimd.memset(future[:, :, :], 0.0).then_inc(const_step, 1)
            nc.gpsimd.memset(head_sel[:, :, :], 0.0).then_inc(const_step, 1)
            nc.gpsimd.memset(nmax[:, :, :], 0.0).then_inc(att_consts, 1)
            for i in range(2):
                nc.gpsimd.memset(v_sb[i][:, :, :, :], 0.0).then_inc(const_step, 1)
            pool.wait_ge(const_step, 8)
            nc.gpsimd.affine_select(out=ident_b[:, :], in_=ident_b[:, :], compare_op=ALU.not_equal, fill=1.0,
                                    base=0, pattern=[[-1, P]], channel_multiplier=1).then_inc(att_consts, 1)
            nc.gpsimd.affine_select(out=future[:, :, :], in_=future[:, :, :], compare_op=ALU.is_ge, fill=NEG,
                                    base=0, pattern=[[0, 4], [-1, P]], channel_multiplier=1).then_inc(att_consts, 1)
            for part in range(3):
                nc.gpsimd.affine_select(out=head_sel[:, :, :], in_=head_sel[:, :, :], compare_op=ALU.not_equal, fill=1.0,
                                        base=-part * HEADS, pattern=[[-1, HEADS], [0, P]], channel_multiplier=1)\
                    .then_inc(const_step, 1)
                pool.wait_ge(const_step, 9 + part)
            for i in range(2):
                nc.gpsimd.memset(v_sb[i][:, :, :, D:D + 1], 1.0).then_inc(att_consts, 1)
            for n, st in enumerate(stages):
                if st == "ffn":
                    ffn_pool(pool, stages[:n].count("ffn"))
                else:
                    attn_pool(pool)

        def ffn_tensor(pe, f):
            s = ffn[f]
            logits = bank[2]

            def route_transpose(u, t):
                pe.wait_ge(s["xn_ready"], t + 1)
                for c in range(HC):
                    last = nc.tensor.transpose(bank[u][:, c * P:(c + 1) * P], xn[:, u, c * P:(c + 1) * P], ident[:, :])
                last.then_inc(s["xn_transposed"], 1)

            def route_logits(u, t):
                pe.wait_ge(s["xnT_ready"], t + 1)
                for c in range(HC):
                    last = nc.tensor.matmul(logits[:, bass.ds(t * E, E)], xnT[:, u, c, :], gwT[:, c, :],
                                            start=(c == 0), stop=(c == HC - 1))
                last.then_inc(s["logits_done"], 1)

            with pe.Fori(0, NT // 2) as k:
                for u in range(2):
                    route_transpose(u, k * 2 + u)
                    route_logits(u, k * 2 + u)
            pe.wait_ge(s["picks_ready"], 1)
            picks_v = picks[:, :, :].rearrange("p t e -> p (t e)")
            nc.tensor.matmul(bank[3][:, :], tri[:, :], picks_v, start=True, stop=True)
            nc.tensor.matmul(bank[4][:, :], ones[:, :], picks_v, start=True, stop=True).then_inc(s["counts_done"], 1)

            def transpose_in(r, k, loaded):
                u = r % 2
                j = k * RING + r
                pe.wait_ge(s["xe_loaded"][r], 16 * loaded)
                for c in range(HC):
                    last = nc.tensor.transpose(bank[u][:, c * P:(c + 1) * P], xe[:, r, c * P:(c + 1) * P], ident[:, :])
                last.then_inc(s["xe_transposed"], 1)

            def gate_up_mm(r, j, e):
                u = r % 2
                pe.wait_ge(s["xeT_ready"], j + 1)
                for c in range(HC):
                    last = nc.tensor.matmul(bank[2 + u][:, 0:2 * I], xeT[:, u, c, :], wgu_sb[:, e, c, :],
                                            start=(c == 0), stop=(c == HC - 1))
                last.then_inc(s["gu_done"], 1)

            def transpose_hid(r, j):
                u = r % 2
                pe.wait_ge(s["hid_ready"], j + 1)
                nc.tensor.transpose(bank[4 + u][:, 0:P], hid[:, u, :], ident[:, :]).then_inc(s["hid_transposed"], 1)

            def down_mm(u, j, e):
                pe.wait_ge(s["hidT_ready"], j + 1)
                nc.tensor.matmul(bank[6 + u][:, 0:H], hidT[:, u, :], wd_sb[:, e, :], start=True, stop=True).then_inc(s["down_done"], 1)

            pe.wait_ge(s["eid_ready"], 1)
            if f == 0:
                pe.wait_ge(wgu_loaded, 16 * HC * (E // 4))
                pe.wait_ge(wd_loaded, 16 * (E // 4))

            def rounds(k, before, after):
                e = [pe.value_load(eid[0:1, bass.ds(k * RING + r, 1)], min_val=0, max_val=E - 1) for r in range(RING)]
                for r in range(RING):
                    j = k * RING + r
                    gate_up_mm(r, j, e[r])
                    if after or r < RING - 1:
                        n = (r + 1) % RING
                        transpose_in(n, k + (r + 1) // RING, k + (r + 1) // RING + 1)
                    if before or r > 0:
                        down_mm((r + 1) % 2, j - 1, e_prev[0] if r == 0 else e[r - 1])
                    transpose_hid(r, j)
                return e[RING - 1]

            transpose_in(0, 0, 1)
            e_prev = [None]
            rounds_first = rounds(0, False, True)
            with pe.Fori(1, NK - 1) as k:
                e_prev[0] = pe.value_load(eid[0:1, bass.ds(k * RING - 1, 1)], min_val=0, max_val=E - 1)
                rounds(k, True, True)
            e_prev[0] = pe.value_load(eid[0:1, bass.ds((NK - 1) * RING - 1, 1)], min_val=0, max_val=E - 1)
            e_last = rounds(NK - 1, True, False)
            down_mm((RING - 1) % 2, NE_T - 1, e_last)

        @block.tensor
        def _(pe):
            pe.wait_ge(consts, 8)
            pe.wait_ge(gw_loaded, 16)
            for c in range(HC):
                last = nc.tensor.transpose(bank[7][:, c * E:(c + 1) * E], gw_sb[:, c * P:(c + 1) * P], ident[0:E, 0:E])
            last.then_inc(gwT_made, 1)
            pe.wait_ge(gwT_ready, 1)
            for n, st in enumerate(stages):
                if st == "ffn":
                    ffn_tensor(pe, stages[:n].count("ffn"))
                else:
                    attn_tensor(pe)

        def ffn_scalar(act, f):
            s = ffn[f]
            act.wait_ge(s["var_ready"], 1)
            nc.scalar.activation(std[:, :], var[:, :], ACT.Sqrt).then_inc(s["std_ready"], 1)
            with act.Fori(0, NT // 2) as k:
                for u in range(2):
                    act.wait_ge(s["xn_transposed"], k * 2 + u + 1)
                    nc.scalar.activation(xnT[:, u, :, :].rearrange("p c n -> p (c n)"), bank[u][:, 0:H],
                                         ACT.Copy).then_inc(s["xnT_ready"], 1)
            act.wait_ge(s["logits_done"], NT)
            nc.scalar.activation(prob[:, :, :].rearrange("p t e -> p (t e)"), bank[2][:, :], ACT.Sigmoid).then_inc(s["prob_ready"], 1)

            def evac_in(u, j):
                act.wait_ge(s["xe_transposed"], j + 1)
                nc.scalar.activation(xeT[:, u, :, :].rearrange("p c n -> p (c n)"), bank[u][:, 0:H],
                                     ACT.Copy).then_inc(s["xeT_ready"], 1)

            def silu_gate(u, j):
                act.wait_ge(s["gu_done"], j + 1)
                nc.scalar.activation(silu[:, u, :], bank[2 + u][:, 0:I], ACT.Silu).then_inc(s["silu_ready"], 1)

            evac_in(0, 0)
            with act.Fori(0, NK - 1) as k:
                for r in range(RING):
                    silu_gate(r % 2, k * RING + r)
                    evac_in((r + 1) % 2, k * RING + r + 1)
            for r in range(RING):
                silu_gate(r % 2, (NK - 1) * RING + r)
                if r < RING - 1:
                    evac_in((r + 1) % 2, (NK - 1) * RING + r + 1)

        @block.scalar
        def _(act):
            act.dma_start(gw_sb[:, :], gate_w).then_inc(gw_loaded, 16)
            act.wait_ge(zero_set, 1)
            gz = grouped_in.rearrange("(n p r) h -> n p (r h)", p=P, r=8)
            for n in range(NE_T // 8):
                act.dma_start(gz[n], zeros[:, :]).then_inc(zero_filled, 16)
            for n, st in enumerate(stages):
                if st == "ffn":
                    ffn_scalar(act, stages[:n].count("ffn"))
                else:
                    attn_scalar(act)

        def row_stats(t):
            return nc.vector.bn_stats(stats[:, t, :], x_sb[:, t, :])

        def layernorm_scale(dve, s):
            nc.vector.memset(mix[0:1, 0:1], 0.0).then_inc(all_stats, 1)
            waited[0] += 1
            dve.wait_ge(all_stats, waited[0])
            nc.vector.tensor_tensor(msum[:, :], stats[:, :, 1], stats[:, :, 4], ALU.add)
            nc.vector.tensor_tensor(mdif[:, :], stats[:, :, 1], stats[:, :, 4], ALU.subtract)
            link(dve, nc.vector.tensor_tensor(vsum[:, :], stats[:, :, 2], stats[:, :, 5], ALU.add))
            nc.vector.tensor_scalar(mean[:, :], msum[:, :], 0.5, None, ALU.mult)
            link(dve, nc.vector.scalar_tensor_tensor(out=mdif[:, :], in0=mdif[:, :], scalar=0.25, in1=mdif[:, :],
                                                     op0=ALU.mult, op1=ALU.mult))
            link(dve, nc.vector.scalar_tensor_tensor(out=vsum[:, :], in0=vsum[:, :], scalar=1.0 / H, in1=mdif[:, :],
                                                     op0=ALU.mult, op1=ALU.add))
            nc.vector.tensor_scalar(var[:, :], vsum[:, :], EPS, None, ALU.add).then_inc(s["var_ready"], 1)
            dve.wait_ge(s["std_ready"], 1)
            nc.vector.reciprocal(rstd[:, :], std[:, :]).then_inc(s["rstd_ready"], 1)
            dve.wait_ge(s["rstd_ready"], 1)

        def normalise(dst, t):
            return nc.vector.tensor_scalar(dst, x_sb[:, t, :], mean[:, bass.ds(t, 1)], rstd[:, bass.ds(t, 1)],
                                           ALU.subtract, ALU.mult)

        def flat(a):
            return a[:, :, :].rearrange("p a b -> p (a b)")

        def over_e(v):
            return v[:, :].unsqueeze(2).broadcast_to([P, NT, E])

        def ffn_vector(dve, f):
            s = ffn[f]
            if f == 0:
                for c in range(LOADS):
                    dve.wait_ge(x_loaded[c], 16)
                    with dve.Fori(c * NT // LOADS, (c + 1) * NT // LOADS) as t:
                        row_stats(t).then_inc(s["stats_done"], 1)
                dve.wait_ge(s["stats_done"], NT)
            layernorm_scale(dve, s)
            for u in range(2):
                normalise(xn[:, u, :], u).then_inc(s["xn_ready"], 1)
            with dve.Fori(1, NT // 2) as k:
                for u in range(2):
                    dve.wait_ge(s["xn_transposed"], k * 2 + u - 1)
                    normalise(xn[:, u, :], k * 2 + u).then_inc(s["xn_ready"], 1)

            dve.wait_ge(s["prob_ready"], 1)
            src = prob
            for j in range(TOPK):
                link(dve, nc.vector.tensor_reduce(top[j][:, :], src[:, :, :], AX.X, ALU.max))
                link(dve, nc.vector.tensor_tensor(eq[:, :, :], src[:, :, :], over_e(top[j]), ALU.is_equal))
                link(dve, nc.vector.tensor_tensor(cand[:, :, :], eq[:, :, :],
                                                  rev[:, :].unsqueeze(1).broadcast_to([P, NT, E]), ALU.mult))
                link(dve, nc.vector.tensor_reduce(first[:, :], cand[:, :, :], AX.X, ALU.max))
                link(dve, nc.vector.tensor_tensor(pick[j][:, :, :], cand[:, :, :], over_e(first), ALU.is_equal))
                if j == 0:
                    link(dve, nc.vector.scalar_tensor_tensor(out=flat(rest), in0=flat(pick[0]), scalar=-2.0, in1=flat(prob),
                                                             op0=ALU.mult, op1=ALU.add))
                    src = rest
            nc.vector.tensor_tensor(picks[:, :, :], pick[0][:, :, :], pick[1][:, :, :], ALU.add).then_inc(s["picks_ready"], 1)
            link(dve, nc.vector.tensor_tensor(wsum[:, :], top[0][:, :], top[1][:, :], ALU.add))
            link(dve, nc.vector.reciprocal(wrec[:, :], wsum[:, :]))
            for j in range(TOPK):
                nc.vector.scalar_tensor_tensor(out=weight[:, :, j], in0=top[j][:, :], scalar=0.5, in1=wrec[:, :],
                                               op0=ALU.mult, op1=ALU.mult)
            dve.wait_ge(s["counts_done"], 1)
            link(dve, nc.vector.tensor_copy(tot[:, :, :], bank[4][:, :].rearrange("p (t e) -> p e t", e=E)))
            link(dve, nc.vector.tensor_tensor_scan(flat(cum), flat(seg), flat(tot), 0.0, ALU.mult, ALU.add))
            link(dve, nc.vector.tensor_tensor(more[:, :, :], cum[:, :, NT - 1:NT].broadcast_to([P, E, NT]),
                                              thr[:, :].unsqueeze(1).broadcast_to([P, E, NT]), ALU.is_gt))
            link(dve, nc.vector.tensor_reduce(ntile[:, :], more[:, :, :], AX.X, ALU.add))
            link(dve, nc.vector.tensor_tensor_scan(end[:, :], one_e[:, :], ntile[:, :], 0.0, ALU.mult, ALU.add))
            nc.vector.tensor_tensor(past[:, :, :], tile_no[:, :].unsqueeze(2).broadcast_to([1, NE_T, E]),
                                    end[0:1, :].unsqueeze(1).broadcast_to([1, NE_T, E]), ALU.is_ge)
            link(dve, nc.vector.tensor_tensor(begin[:, :], end[:, :], ntile[:, :], ALU.subtract))
            link(dve, nc.vector.tensor_reduce(eid_f[:, :], past[:, :, :], AX.X, ALU.add))
            nc.vector.tensor_scalar(eid[:, :], eid_f[:, :], float(E - 1), None, ALU.min).then_inc(s["eid_ready"], 1)
            link(dve, nc.vector.tensor_tensor(slot_e[:, :, :], cum[:, :, :], tot[:, :, :], ALU.subtract))
            link(dve, nc.vector.tensor_scalar(begin[:, :], begin[:, :], float(P), None, ALU.mult))
            link(dve, nc.vector.tensor_tensor(slot_e[:, :, :], slot_e[:, :, :],
                                              begin[:, :].unsqueeze(2).broadcast_to([P, E, NT]), ALU.add))
            link(dve, nc.vector.tensor_tensor(slot_t[:, :, :], bank[3][:, :].rearrange("p (t e) -> p t e", e=E),
                                              slot_e[:, :, :].rearrange("p e t -> p t e"), ALU.add))
            for j in range(TOPK):
                link(dve, nc.vector.tensor_tensor(cand[:, :, :], slot_t[:, :, :], pick[j][:, :, :], ALU.mult))
                link(dve, nc.vector.tensor_reduce(slot_f[:, :, j], cand[:, :, :], AX.X, ALU.add))
            link(dve, nc.vector.tensor_copy(slot[:, :, :], slot_f[:, :, :]))

            def dispatch(r, t, k):
                for j in range(TOPK):
                    nc.vector.tensor_copy(idx[r][j][:, :], slot[:, t, j:j + 1])
                normalise(row_out[r][:, :], t).then_inc(s["rows_ready"], 1)

            for r in range(RING):
                dispatch(r, r, 0)
            with dve.Fori(1, NT // RING) as k:
                for r in range(RING):
                    dve.wait_ge(s["scattered"][r], k * (16 * TOPK))
                    dispatch(r, k * RING + r, k)

            def gated(u, j):
                dve.wait_ge(s["silu_ready"], j + 1)
                nc.vector.tensor_tensor(hid[:, u, :], bank[2 + u][:, I:2 * I], silu[:, u, :], ALU.mult).then_inc(s["hid_ready"], 1)

            def evac_hid(u, j):
                dve.wait_ge(s["hid_transposed"], j + 1)
                nc.vector.tensor_copy(hidT[:, u, :], bank[4 + u][:, 0:P]).then_inc(s["hidT_ready"], 1)

            def evac_out(r, j, k, wait):
                dve.wait_ge(s["down_done"], j + 1)
                if wait:
                    dve.wait_ge(s["ye_stored"][r], k * 16)
                nc.vector.tensor_copy(ye[:, r, :], bank[6 + r % 2][:, 0:H]).then_inc(s["ye_ready"], 1)

            def expert_round(k, first_round):
                for r in range(RING):
                    j = k * RING + r
                    gated(r % 2, j)
                    if r > 0:
                        evac_out(r - 1, j - 1, k, not first_round)
                    elif not first_round:
                        evac_out(RING - 1, j - 1, k - 1, True) if (not isinstance(k, int) or k > 1) else evac_out(RING - 1, j - 1, 0, False)
                    evac_hid(r % 2, j)

            expert_round(0, True)
            expert_round(1, False)
            with dve.Fori(2, NK) as k:
                expert_round(k, False)
            evac_out(RING - 1, NE_T - 1, NK - 1, True)

            def fetch(r, t):
                nc.vector.tensor_copy(idx[r][0][:, :], slot[:, t, 0:1])
                nc.vector.tensor_copy(idx[r][1][:, :], slot[:, t, 1:2]).then_inc(s["idx_ready"], 1)

            def combine(r, t, k):
                dve.wait_ge(s["gathered"][r], (k + 1) * (16 * TOPK))
                nc.vector.scalar_tensor_tensor(out=mix[:, :], in0=got[r][0][:, :], scalar=weight[:, t, 0:1],
                                               in1=x_sb[:, t, :], op0=ALU.mult, op1=ALU.add).then_inc(s["mix_ready"], 1)
                dve.wait_ge(s["mix_ready"], t + 1)
                nc.vector.scalar_tensor_tensor(out=x_sb[:, t, :], in0=got[r][1][:, :], scalar=weight[:, t, 1:2],
                                               in1=mix[:, :], op0=ALU.mult, op1=ALU.add).then_inc(s["x_done"], 1)
                dve.wait_ge(s["x_done"], t + 1)
                if f < NF - 1:
                    row_stats(t)

            for r in range(RING):
                dve.wait_ge(s["scattered"][r], 16 * TOPK * NT // RING)
                fetch(r, r)
            with dve.Fori(0, NT // RING - 1) as k:
                for r in range(RING):
                    combine(r, k * RING + r, k)
                    fetch(r, k * RING + RING + r)
            for r in range(RING):
                combine(r, NT - RING + r, NT // RING - 1)

        @block.vector
        def _(dve):
            dve.wait_ge(gwT_made, 1)
            nc.vector.tensor_copy(gwT[:, :, :].rearrange("p c e -> p (c e)"), bank[7][:, 0:HC * E]).then_inc(gwT_ready, 1)
            dve.wait_ge(consts, 8)
            dve.wait_ge(wqkv_loaded, 16)
            nc.vector.tensor_scalar(wqkv_sb[:, :, 0:H], wqkv_sb[:, :, 0:H], 1.0 / float(D) ** 0.5, None, ALU.mult)\
                .then_inc(wqkv_scaled, 1)
            for n, st in enumerate(stages):
                if st == "ffn":
                    ffn_vector(dve, stages[:n].count("ffn"))
                else:
                    attn_vector(dve)


_INS = ["L0_attn_x", "L0_attn_w_qkv", "L0_attn_w_out", "L0_ffn_gate_w", "L0_ffn_gate_up_proj", "L0_ffn_down_proj"]


def kernel(**inputs):
    import numpy as _np
    import concourse.bacc as _bacc
    from concourse.bass_utils import run_bass_kernel_spmd as _run

    nc = _bacc.Bacc("TRN2", target_bir_lowering=False, num_devices=1)
    arrays, args = {}, []
    for name in _INS:
        a = _np.ascontiguousarray(inputs[name])
        arrays[f"in_{name}_dram"] = a
        args.append(nc.dram_tensor(f"in_{name}_dram", a.shape, mybir.dt.from_np(a.dtype), kind="ExternalInput").ap())
    shape = arrays["in_L0_attn_x_dram"].shape
    args.append(nc.dram_tensor("out_0_dram", shape, F32, kind="ExternalOutput").ap())
    macaron_block(nc, *args)
    r = _run(nc, [arrays], core_ids=[0])
    return r.results[0]["out_0_dram"]
```

```python
import concourse.bass as bass
from concourse import mybir
from contextlib import ExitStack

F32 = mybir.dt.float32
BF16 = mybir.dt.bfloat16
U32 = mybir.dt.uint32
I32 = mybir.dt.int32
ALU = mybir.AluOpType
ACT = mybir.ActivationFunctionType
AX = mybir.AxisListType

P = 128


def macaron_block(nc, x_in, w_qkv, w_out, gate_w, gate_up, down, out, stages=("ffn", "attn", "ffn")):
    B, S, H = x_in.shape
    NT = B * S // P
    HC = H // P
    E = gate_w.shape[0]
    I = down.shape[1]
    TOPK = 2
    NE_T = B * S * TOPK // P + E
    RING = 4
    NK = NE_T // RING
    LOADS = 4
    EPS = 1e-5
    HEADS, D = 16, H // 16
    NEG = -1e30
    SLOTS = 7
    VW = 32
    G = HEADS // 4
    NF = stages.count("ffn")

    x_tiles = x_in.rearrange("b (n p) h -> p (b n) h", p=P)
    out_tiles = out.rearrange("b (n p) h -> p (b n) h", p=P)

    grouped_in = nc.dram_tensor("grouped_in", [NE_T * P, H], F32).ap()
    grouped_out = nc.dram_tensor("grouped_out", [NE_T * P, H], F32).ap()

    ctx = ExitStack()
    with ctx:
        def sb(name, shape, dt=F32):
            return ctx.enter_context(nc.sbuf_tensor(name, shape, dt))

        def sem(name):
            return ctx.enter_context(nc.semaphore(name))

        bank = [ctx.enter_context(nc.psum_tensor(f"bank{i}", [P, 512], F32)) for i in range(8)]

        shared = sb("shared", [P, 4 * HEADS * S // 2])
        taken = [0]

        def lay(n, dims, **sizes):
            taken[0] += n
            assert taken[0] <= 4 * HEADS * S // 2
            return shared[:, taken[0] - n:taken[0]].rearrange(dims, **sizes)

        x_sb = sb("x_sb", [P, NT, H])
        wgu_sb = sb("wgu_sb", [P, E, HC, 2 * I])
        wd_sb = sb("wd_sb", [P, E, H])
        gw_sb = sb("gw_sb", [E, H])
        gwT = sb("gwT", [P, HC, E])
        ident = sb("ident", [P, P])
        tri = sb("tri", [P, P], BF16)
        ones = sb("ones", [P, P], BF16)
        rev = sb("rev", [P, E])
        thr = sb("thr", [P, NT])
        tile_no = sb("tile_no", [1, NE_T])
        one_e = sb("one_e", [P, E])
        seg = sb("seg", [P, E, NT])
        stats = sb("stats", [P, NT, 6])
        msum = sb("msum", [P, NT])
        mdif = sb("mdif", [P, NT])
        vsum = sb("vsum", [P, NT])
        mean = sb("mean", [P, NT])
        var = sb("var", [P, NT])
        std = sb("std", [P, NT])
        rstd = sb("rstd", [P, NT])
        xn = sb("xn", [P, 2, H])
        xnT = sb("xnT", [P, 2, HC, P])
        prob = lay(NT * E, "p (t e) -> p t e", e=E)
        top = [sb(f"top{k}", [P, NT]) for k in range(TOPK)]
        eq = lay(NT * E, "p (t e) -> p t e", e=E)
        cand = lay(NT * E, "p (t e) -> p t e", e=E)
        first = sb("first", [P, NT])
        pick = [lay(NT * E, "p (t e) -> p t e", e=E) for k in range(TOPK)]
        rest = lay(NT * E, "p (t e) -> p t e", e=E)
        picks = sb("picks", [P, NT, E], BF16)
        wsum = sb("wsum", [P, NT])
        wrec = sb("wrec", [P, NT])
        weight = sb("weight", [P, NT, TOPK])
        tot = lay(E * NT, "p (e t) -> p e t", e=E)
        cum = lay(E * NT, "p (e t) -> p e t", e=E)
        more = lay(E * NT, "p (e t) -> p e t", e=E)
        ntile = sb("ntile", [P, E])
        end = sb("end", [P, E])
        begin = sb("begin", [P, E])
        slot_e = more
        slot_t = lay(NT * E, "p (t e) -> p t e", e=E)
        slot_f = sb("slot_f", [P, NT, TOPK])
        slot = sb("slot", [P, NT, TOPK], U32)
        past = sb("past", [1, NE_T, E])
        eid_f = sb("eid_f", [1, NE_T])
        eid = sb("eid", [1, NE_T], I32)
        wqkv_sb = sb("wqkv_sb", [P, HC, 3 * H])
        wout_sb = sb("wout_sb", [P, HC, H])
        ident_b = sb("ident_b", [P, P], BF16)
        future = sb("future", [P, 4, P], BF16)
        head_sel = sb("head_sel", [P, HEADS, P], BF16)
        an = sb("an", [P, 2, H])
        anT = sb("anT", [P, HC, S])
        stack = [sb(f"stack{u}", [P, 2, HEADS, SLOTS, D], BF16) for u in range(2)]
        left = [sb(f"left{u}", [P, 2, HEADS, D]) for u in range(2)]
        half = HEADS * S // 2
        qT, kT = ([shared[0:SLOTS * D, (2 * a + i) * half:(2 * a + i + 1) * half].bitcast(BF16)
                   .rearrange("p (h n) -> p h n", h=HEADS) for i in range(2)] for a in range(2))
        v_sb = [sb(f"v_sb{i}", [P, 2, HEADS, VW]) for i in range(2)]
        mx = sb("mx", [P, 2, HEADS])
        nleft = sb("nleft", [P, 2, HEADS])
        nmax = sb("nmax", [P, 2, P], BF16)
        nmaxT = [sb(f"nmaxT{i}", [P, S], BF16) for i in range(2)]
        pr0 = [sb(f"pr0_{i}", [P, 4, S]) for i in range(2)]
        pr1 = [sb(f"pr1_{i}", [P, 4, P]) for i in range(2)]
        oT = sb("oT", [P, HEADS // 4, S])
        rsum = sb("rsum", [P, 2, HEADS])
        att = sb("att", [P, 2, H])
        attT = sb("attT", [P, 2, HC, P])
        idx = [[sb(f"idx{r}_{k}", [P, 1], U32) for k in range(TOPK)] for r in range(RING)]
        gathered_rows = lay(RING * TOPK * H, "p (r k h) -> p r k h", r=RING, k=TOPK)
        got = [[gathered_rows[:, r, k, :] for k in range(TOPK)] for r in range(RING)]
        zeros = gathered_rows.rearrange("p r k h -> p (r k h)")
        xe = lay(RING * H, "p (r h) -> p r h", r=RING)
        row_out = [xe[:, r, :] for r in range(RING)]
        xeT = sb("xeT", [P, 2, HC, P])
        silu = sb("silu", [P, 2, I])
        hid = sb("hid", [P, 2, I])
        hidT = sb("hidT", [P, 2, P])
        ye = sb("ye", [P, RING, H])
        mix = sb("mix", [P, H])

        x_loaded = [sem(f"x_loaded{c}") for c in range(LOADS)]
        gw_loaded = sem("gw_loaded")
        wgu_loaded = sem("wgu_loaded")
        wd_loaded = sem("wd_loaded")
        zero_set = sem("zero_set")
        zero_filled = sem("zero_filled")
        consts = sem("consts")
        const_step = sem("const_step")
        gwT_made = sem("gwT_made")
        gwT_ready = sem("gwT_ready")
        all_stats = sem("all_stats")
        step = sem("step")
        stored = sem("stored")
        pool_turn = sem("pool_turn")

        def ffn_sems(f):
            names = ("stats_done", "var_ready", "std_ready", "rstd_ready", "xn_ready", "xn_transposed", "xnT_ready",
                     "logits_done", "prob_ready", "picks_ready", "counts_done", "eid_ready", "rows_ready",
                     "xe_transposed", "xeT_ready", "gu_done", "silu_ready", "hid_ready", "hid_transposed",
                     "hidT_ready", "down_done", "ye_ready", "idx_ready", "mix_ready", "x_done")
            rings = ("scattered", "xe_loaded", "ye_stored", "gathered")
            found = {n: sem(f"{n}_f{f}") for n in names}
            found.update({n: [sem(f"{n}{r}_f{f}") for r in range(RING)] for n in rings})
            return found

        at = {n: sem(f"{n}_at") for n in (
            "var_ready", "std_ready", "rstd_ready", "an_ready", "an_transposed", "anT_ready", "qk_done", "hi_ready",
            "left_ready", "mid_ready", "low_ready", "parts_copied", "highs_copied", "v_done", "v_ready",
            "fill_done", "fill_act", "fill_dve", "score_done", "max_ready", "nmax_step", "nmax_ready", "nmax_transposed",
            "nmaxT_ready", "scoreT_done", "exp_ready", "masked", "pv_done", "oT_ready", "o_transposed",
            "rsum_ready", "att_ready", "att_transposed", "attT_ready", "proj_done", "x_done")}
        wqkv_loaded = sem("wqkv_loaded")
        wqkv_scaled = sem("wqkv_scaled")
        wout_loaded = sem("wout_loaded")
        att_consts = sem("att_consts")
        ffn = [ffn_sems(f) for f in range(NF)]
        count, waited = [0], [0]

        def link(dve, ins):
            count[0] += 1
            ins.then_inc(step, 1)
            dve.wait_ge(step, count[0])

        def later(eng, s, b, per, n):
            if isinstance(b, int) and per * b + n <= 0:
                return
            eng.wait_ge(s, b * per + n)

        def exists(j):
            return not isinstance(j, int) or 0 <= j < NE_T

        block = ctx.enter_context(nc.Block())

        NORM, F, FILL, SCORE = "norm", "front", "fill", "score"
        T, PV, UN, TR, PR = "scoreT", "pv", "untranspose", "transpose", "project"
        TURN = [(-1, (F, "negate")), (0, (F, "qk0")), (-1, (F, "max")), (0, (F, "qk1")), (-1, (T, 0)), (-1, (T, 1)), (0, (F, "v")),
                (-1, (T, 2)), (-1, (T, 3)), (0, (FILL, 0)), (0, (FILL, 1)), (-1, (T, 4)), (0, (FILL, 2)), (-1, (PV, 0)),
                (0, (FILL, 3)), (-1, (T, 5)), (0, (FILL, 4)), (-1, (T, 6)), (0, (FILL, 5)), (-1, (T, 7)), (-1, (PV, 1)),
                (0, (FILL, 6)), (-1, (T, 8)), (0, (FILL, 7)), (-1, (T, 9)), (1, (NORM, 0)), (-1, (PV, 2)), (-1, (T, 10)),
                (0, (SCORE, 0)), (-1, (T, 11)), (0, (SCORE, 1)), (0, (SCORE, 2)), (-1, (PV, 3)), (0, (SCORE, 3)),
                (0, (SCORE, 4)), (-1, (UN, 0)), (-1, (UN, 1)), (0, (SCORE, 5)), (0, (SCORE, 6)), (-1, (TR, 0)), (-1, (TR, 1)),
                (0, (SCORE, 7)), (0, (SCORE, 8)), (-1, (PR, 0)), (-1, (PR, 1)), (0, (SCORE, 9)), (0, (SCORE, 10)),
                (0, (SCORE, 11))]

        def batches(eng, part):
            def turn(b, i):
                for after, st in TURN:
                    if not isinstance(b, int) or 0 <= b + after < B:
                        part(st, b + after, (i + after) % 2)

            turn(-1, 1)
            turn(0, 0)
            turn(1, 1)
            with eng.Fori(1, B // 2 - 1) as m:
                for i in range(2):
                    turn(m * 2 + i, i)
            for b in range(B - 2, B + 1):
                turn(b, b)

        bankA, bankB, bankC = bank[5], bank[6], bank[7]

        def fill_of(i):
            return i // 4, i // 2 % 2, i % 2 * 8, (bankA, bankB)[i % 2]

        FILL_ACT = (2, 6)

        def wait_fills(eng, b, n):
            later(eng, at["fill_act"], b, 2, sum(i < n for i in FILL_ACT))
            later(eng, at["fill_dve"], b, 6, sum(i not in FILL_ACT for i in range(n)))

        def score_of(n):
            return (0, 4 * n, 4) if n < G else (1, 2 * (n - G), 2)

        def scoreT_of(n):
            g, i = n // 3, n % 3
            return (0, 4 * g + 2 * i, 2) if i < 2 else (1, 4 * g, 4)

        def attn_pool(pool):
            def part(st, b, p):
                kind, n = st
                if kind == "scoreT" and n % 3:
                    g, second = n // 3, n % 3 == 2
                    later(pool, at["exp_ready"], b, 3 * G, n + 1)
                    pool.sem_inc(pool_turn, 1)
                    m = (pr1 if second else pr0)[g % 2][:, :, 0:P]
                    nc.gpsimd.affine_select(out=m, in_=m, compare_op=ALU.is_ge, fill=0.0, base=0,
                                            pattern=[[0, 4], [1, P]], channel_multiplier=-1).then_inc(at["masked"], 1)
            batches(pool, part)

        def attn_tensor(pe):
            pe.wait_ge(wqkv_scaled, 1)
            pe.wait_ge(wout_loaded, 16)
            pe.wait_ge(att_consts, 5)

            def qk_product(u, b, dst):
                for c in range(HC):
                    last = nc.tensor.matmul(dst[:, :], anT[:, c, u * P:(u + 1) * P], wqkv_sb[:, c, 0:2 * H],
                                            start=(c == 0), stop=(c == HC - 1))
                last.then_inc(at["qk_done"], 1)

            def part(st, b, p):
                kind, n = st
                if kind == "norm":
                    later(pe, at["an_ready"], b, 2, 2)
                    wait_fills(pe, b, 0)
                    for u in range(2):
                        for c in range(HC):
                            last = nc.tensor.transpose(bankA[:, c * S + u * P:c * S + (u + 1) * P],
                                                       an[:, u, c * P:(c + 1) * P], ident[:, :])
                    last.then_inc(at["an_transposed"], 1)
                elif st == ("front", "qk0"):
                    later(pe, at["anT_ready"], b, 1, 1)
                    wait_fills(pe, b, 0)
                    qk_product(0, b, bankB)
                elif st == ("front", "qk1"):
                    qk_product(1, b, bankA)
                elif st == ("front", "v"):
                    later(pe, at["left_ready"], b, 2, 1)
                    for u in range(2):
                        for c in range(HC):
                            last = nc.tensor.matmul(bankB[:, u * H:(u + 1) * H], anT[:, c, u * P:(u + 1) * P],
                                                    wqkv_sb[:, c, 2 * H:3 * H], start=(c == 0), stop=(c == HC - 1))
                    last.then_inc(at["v_done"], 1)
                elif kind == "fill":
                    u, qk, h0, dst = fill_of(n)
                    later(pe, at["parts_copied"], b, 2, u + 1)
                    later(pe, at["highs_copied"], b, 2, u + 1)
                    if n == 0:
                        later(pe, at["left_ready"], b, 2, 2)
                    elif n == 1:
                        later(pe, at["v_ready"], b, 1, 1)
                    else:
                        wait_fills(pe, b, n - 1)
                    for i in range(8):
                        last = nc.tensor.transpose(dst[:, :].bitcast(BF16)[0:SLOTS * D, i * P:(i + 1) * P],
                                                   stack[u][:, qk, h0 + i, :, :].rearrange("p s d -> p (s d)"), ident_b[:, :])
                    last.then_inc(at["fill_done"], 1)
                elif kind == "score":
                    u, h0, nh = score_of(n)
                    wait_fills(pe, b, 4 * (u + 1))
                    later(pe, at["max_ready"], b, 3 * G, n - 1)
                    dst, w = bank[3 + n % 2], P * (u + 1)
                    for i in range(nh):
                        nc.tensor.matmul(dst[:, i * w:(i + 1) * w], qT[p][:, h0 + i, u * P:(u + 1) * P], kT[p][:, h0 + i, 0:w],
                                         start=(i == 0), stop=False, skip_group_check=True)
                    diag = dst[:, :].rearrange("p (h k) -> p h k", k=w)[:, :, u * P:(u + 1) * P]
                    nc.tensor.matmul(diag, ident_b[:, :], future[:, 0:nh, :], start=False, stop=True,
                                     skip_group_check=True).then_inc(at["score_done"], 1)
                elif st == ("front", "max"):
                    later(pe, at["nmax_ready"], b, 1, 1)
                    later(pe, at["x_done"], b, 2, 0)
                    for u in range(2):
                        last = nc.tensor.transpose(bankC[:, :].bitcast(BF16)[:, u * P:(u + 1) * P], nmax[:, u, :], ident_b[:, :])
                    last.then_inc(at["nmax_transposed"], 1)
                elif kind == "scoreT":
                    kt, h0, nh = scoreT_of(n)
                    later(pe, at["nmaxT_ready"], b, 1, 1)
                    later(pe, at["exp_ready"], b, 3 * G, n - 2)
                    if n < 3:
                        later(pe, at["x_done"], b, 2, 0)
                    dst, w = bank[n % 3], S - kt * P
                    for i in range(nh):
                        h = h0 + i
                        nc.tensor.matmul(dst[:, i * w:(i + 1) * w], kT[p][:, h, kt * P:(kt + 1) * P], qT[p][:, h, kt * P:S],
                                         start=(i == 0), stop=False, skip_group_check=True)
                        last = nc.tensor.matmul(dst[:, i * w:(i + 1) * w], head_sel[:, h, :], nmaxT[p][:, kt * P:S],
                                                start=False, stop=True, skip_group_check=True)
                    last.then_inc(at["scoreT_done"], 1)
                elif kind == "pv":
                    later(pe, at["masked"], b, 2 * G, 2 * n + 2)
                    later(pe, at["oT_ready"], b, G, n)
                    cols = n % 2 * S
                    for kt in range(2):
                        for j in range(4):
                            rhs = pr0[n % 2][:, j, :] if kt == 0 else pr1[n % 2][:, j, :]
                            last = nc.tensor.matmul(bankC[j * VW:(j + 1) * VW, cols + kt * P:cols + S],
                                                    v_sb[p][:, kt, 4 * n + j, :], rhs, start=(kt == 0), stop=(kt == 1),
                                                    skip_group_check=True)
                    last.then_inc(at["pv_done"], 1)
                elif kind == "untranspose":
                    later(pe, at["oT_ready"], b, G, G)
                    later(pe, at["exp_ready"], b, 3 * G, 3 * G)
                    for g in range(G):
                        last = nc.tensor.transpose(bank[n][:, g * P:(g + 1) * P], oT[:, g, n * P:(n + 1) * P], ident[:, :])
                    last.then_inc(at["o_transposed"], 1)
                elif kind == "transpose":
                    later(pe, at["att_ready"], b, 2, n + 1)
                    for c in range(HC):
                        last = nc.tensor.transpose((bankC, bank[2])[n][:, c * P:(c + 1) * P], att[:, n, c * P:(c + 1) * P], ident[:, :])
                    last.then_inc(at["att_transposed"], 1)
                elif kind == "project":
                    later(pe, at["attT_ready"], b, 2, n + 1)
                    for c in range(HC):
                        last = nc.tensor.matmul(bank[n][:, 0:H], attT[:, n, c, :], wout_sb[:, c, :], start=(c == 0), stop=(c == HC - 1))
                    last.then_inc(at["proj_done"], 1)
            batches(pe, part)

        def attn_scalar(act):
            act.wait_ge(at["var_ready"], 1)
            nc.scalar.activation(std[:, :], var[:, :], ACT.Sqrt).then_inc(at["std_ready"], 1)

            def part(st, b, p):
                kind, n = st
                if kind == "norm":
                    later(act, at["an_transposed"], b, 1, 1)
                    nc.scalar.copy(anT[:, :, :].rearrange("p c n -> p (c n)"), bankA[:, :]).then_inc(at["anT_ready"], 1)
                elif kind == "front" and n in ("qk0", "qk1"):
                    u = int(n[2])
                    src = (bankB, bankA)[u]
                    later(act, at["qk_done"], b, 2, u + 1)
                    nc.scalar.copy(stack[u][:, :, :, 0, :].rearrange("p a h d -> p (a h) d"),
                                         src[:, :].rearrange("p (h d) -> p h d", d=D)).then_inc(at["hi_ready"], 1)
                    later(act, at["hi_ready"], b, 2, u + 1)
                    for qk, to in ((0, 3), (1, 5)):
                        last = nc.scalar.copy(stack[u][:, qk, :, to:to + 2, :],
                                              stack[u][:, qk, :, 0:1, :].broadcast_to([P, HEADS, 2, D]))
                    last.then_inc(at["highs_copied"], 1)
                    later(act, at["left_ready"], b, 2, u + 1)
                    nc.scalar.copy(stack[u][:, :, :, 1, :].rearrange("p a h d -> p (a h) d"),
                                         left[u][:, :, :, :].rearrange("p a h d -> p (a h) d")).then_inc(at["mid_ready"], 1)
                elif st == ("front", "v"):
                    later(act, at["v_done"], b, 1, 1)
                    nc.scalar.copy(v_sb[p][:, :, :, 0:D], bankB[:, :].rearrange("p (u h d) -> p u h d", u=2, d=D))\
                        .then_inc(at["v_ready"], 1)
                elif kind == "pv":
                    later(act, at["pv_done"], b, G, n + 1)
                    nc.scalar.copy(oT[:, n, :], bankC[:, n % 2 * S:(n % 2 + 1) * S]).then_inc(at["oT_ready"], 1)
                elif kind == "fill" and n in FILL_ACT:
                    u, qk, h0, src = fill_of(n)
                    later(act, at["fill_done"], b, 8, n + 1)
                    dst = (qT, kT)[qk][p]
                    nc.scalar.copy(dst[:, h0:h0 + 8, u * P:(u + 1) * P],
                                         src[:, :].bitcast(BF16)[0:SLOTS * D, :].rearrange("p (h n) -> p h n", n=P)).then_inc(at["fill_act"], 1)
                elif st == ("front", "max"):
                    later(act, at["nmax_transposed"], b, 1, 1)
                    nc.scalar.copy(nmaxT[p][:, :], bankC[:, :].bitcast(BF16)[:, 0:S]).then_inc(at["nmaxT_ready"], 1)
                elif kind == "scoreT":
                    kt, h0, nh = scoreT_of(n)
                    g = n // 3
                    later(act, at["scoreT_done"], b, 3 * G, n + 1)
                    if n % 3 == 0:
                        later(act, at["pv_done"], b, G, g - 1)
                    dst = pr1[g % 2][:, :, :] if kt else pr0[g % 2][:, h0 % 4:h0 % 4 + 2, :]
                    nc.scalar.activation(dst.rearrange("p h n -> p (h n)"), bank[n % 3][:, :], ACT.Exp).then_inc(at["exp_ready"], 1)
                elif kind == "transpose":
                    later(act, at["att_transposed"], b, 2, n + 1)
                    nc.scalar.copy(attT[:, n, :, :].rearrange("p c n -> p (c n)"), (bankC, bank[2])[n][:, 0:H]).then_inc(at["attT_ready"], 1)
            batches(act, part)

        def attn_vector(dve):
            layernorm_scale(dve, at)

            def split(u, b):
                src = (bankB, bankA)[u]
                later(dve, at["hi_ready"], b, 2, u + 1)
                nc.vector.tensor_tensor(left[u][:, :, :, :].rearrange("p a h d -> p (a h) d"),
                                        src[:, :].rearrange("p (h d) -> p h d", d=D),
                                        stack[u][:, :, :, 0, :].rearrange("p a h d -> p (a h) d"), ALU.subtract)\
                    .then_inc(at["left_ready"], 1)

            def split_low(u, b):
                later(dve, at["mid_ready"], b, 2, u + 1)
                nc.vector.tensor_tensor(stack[u][:, :, :, 2, :].rearrange("p a h d -> p (a h) d"),
                                        left[u][:, :, :, :].rearrange("p a h d -> p (a h) d"),
                                        stack[u][:, :, :, 1, :].rearrange("p a h d -> p (a h) d"), ALU.subtract)\
                    .then_inc(at["low_ready"], 1)
                later(dve, at["low_ready"], b, 2, u + 1)
                for qk, to in ((0, 5), (1, 3)):
                    last = nc.vector.tensor_copy(stack[u][:, qk, :, to:to + 2, :], stack[u][:, qk, :, 1:3, :])
                last.then_inc(at["parts_copied"], 1)

            def part(st, b, p):
                kind, n = st
                if kind == "norm":
                    later(dve, at["an_transposed"], b, 1, 0)
                    for u in range(2):
                        normalise(an[:, u, :], b * 2 + u).then_inc(at["an_ready"], 1)
                elif st == ("front", "qk0"):
                    split(0, b)
                elif st == ("front", "qk1"):
                    split(1, b)
                    split_low(0, b)
                elif st == ("front", "v"):
                    split_low(1, b)
                elif kind == "fill" and n not in FILL_ACT:
                    u, qk, h0, src = fill_of(n)
                    later(dve, at["fill_done"], b, 8, n + 1)
                    dst = (qT, kT)[qk][p]
                    nc.vector.tensor_copy(dst[:, h0:h0 + 8, u * P:(u + 1) * P],
                                          src[:, :].bitcast(BF16)[0:SLOTS * D, :].rearrange("p (h n) -> p h n", n=P))\
                        .then_inc(at["fill_dve"], 1)
                elif kind == "score":
                    u, h0, nh = score_of(n)
                    later(dve, at["score_done"], b, 3 * G, n + 1)
                    nc.vector.tensor_reduce(mx[:, u, h0:h0 + nh], bank[3 + n % 2][:, :].rearrange("p (h k) -> p h k", h=nh),
                                            AX.X, ALU.max).then_inc(at["max_ready"], 1)
                elif st == ("front", "negate"):
                    later(dve, at["max_ready"], b, 3 * G, 3 * G)
                    nc.vector.tensor_scalar(nmax[:, :, 0:HEADS], mx[:, :, :], -1.0, None, ALU.mult).then_inc(at["nmax_step"], 1)
                    later(dve, at["nmax_step"], b, 3, 1)
                    nc.vector.scalar_tensor_tensor(out=nleft[:, :, :], in0=mx[:, :, :], scalar=-1.0, in1=nmax[:, :, 0:HEADS],
                                                   op0=ALU.mult, op1=ALU.subtract).then_inc(at["nmax_step"], 1)
                    later(dve, at["nmax_step"], b, 3, 2)
                    nc.vector.tensor_copy(nmax[:, :, HEADS:2 * HEADS], nleft[:, :, :]).then_inc(at["nmax_step"], 1)
                    later(dve, at["nmax_step"], b, 3, 3)
                    nc.vector.tensor_tensor(nmax[:, :, 2 * HEADS:3 * HEADS], nleft[:, :, :], nmax[:, :, HEADS:2 * HEADS],
                                            ALU.subtract).then_inc(at["nmax_ready"], 1)
                elif kind == "untranspose":
                    later(dve, at["o_transposed"], b, 2, n + 1)
                    o = bank[n][:, :].rearrange("p (h d) -> p h d", d=VW)
                    nc.vector.reciprocal(rsum[:, n, :], o[:, :, D]).then_inc(at["rsum_ready"], 1)
                    later(dve, at["rsum_ready"], b, 2, n + 1)
                    nc.vector.tensor_tensor(att[:, n, :].rearrange("p (h d) -> p h d", d=D), o[:, :, 0:D],
                                            rsum[:, n, :].unsqueeze(2).broadcast_to([P, HEADS, D]), ALU.mult).then_inc(at["att_ready"], 1)
                elif kind == "project":
                    later(dve, at["proj_done"], b, 2, n + 1)
                    t = b * 2 + n
                    nc.vector.tensor_tensor(x_sb[:, t, :], bank[n][:, 0:H], x_sb[:, t, :], ALU.add).then_inc(at["x_done"], 1)
                    later(dve, at["x_done"], b, 2, n + 1)
                    row_stats(t)
            batches(dve, part)

        def ffn_sync(sp, f):
            s = ffn[f]

            def load(r, k):
                sp.dma_start(xe[:, r, :], grouped_in[bass.ds((k * RING + r) * P, P), :]).then_inc(s["xe_loaded"][r], 16)

            def store(r, k):
                sp.wait_ge(s["ye_ready"], k * RING + r + 1)
                sp.dma_start(grouped_out[bass.ds((k * RING + r) * P, P), :], ye[:, r, :]).then_inc(s["ye_stored"][r], 16)

            for r in range(RING):
                sp.wait_ge(s["scattered"][r], 16 * TOPK * NT // RING)
            for r in range(RING):
                load(r, 0)

            def turn(k, rs):
                for r in rs:
                    if exists(k * RING + r + RING):
                        sp.wait_ge(s["xe_transposed"], k * RING + r + 1)
                        load(r, k + 1)
                    if exists(k * RING + r - 2):
                        store((r - 2) % RING, k if r >= 2 else k - 1)

            turn(0, range(RING))
            with sp.Fori(1, NK - 1) as k:
                turn(k, range(RING))
            turn(NK - 1, range(RING + 2))

        @block.sync
        def _(sp):
            step_ = NT // LOADS
            for c in range(LOADS):
                sp.dma_start(x_sb[:, c * step_:(c + 1) * step_, :], x_tiles[:, c * step_:(c + 1) * step_, :]).then_inc(x_loaded[c], 16)
            for g in range(0, E, 4):
                if g == 4:
                    sp.dma_start(wqkv_sb[:, :, :], w_qkv.rearrange("(c p) f -> p c f", p=P)).then_inc(wqkv_loaded, 16)
                    sp.dma_start(wout_sb[:, :, :], w_out.rearrange("(c p) f -> p c f", p=P)).then_inc(wout_loaded, 16)
                for c in range(HC):
                    sp.dma_start(wgu_sb[:, g:g + 4, c, :],
                                 gate_up[g:g + 4, c * P:(c + 1) * P, :].rearrange("e p f -> p e f")).then_inc(wgu_loaded, 16)
                sp.dma_start(wd_sb[:, g:g + 4, :], down[g:g + 4].rearrange("e i h -> i e h")).then_inc(wd_loaded, 16)
            for n, st in enumerate(stages):
                if st == "ffn":
                    ffn_sync(sp, stages[:n].count("ffn"))
            s = ffn[NF - 1]
            with sp.Fori(0, NT // 2) as k:
                sp.wait_ge(s["x_done"], k * 2 + 2)
                sp.dma_start(out_tiles[:, bass.ds(k * 2, 2), :], x_sb[:, bass.ds(k * 2, 2), :]).then_inc(stored, 16)
            sp.wait_ge(stored, 16 * (NT // 2))

        def ffn_pool(pool, f):
            s = ffn[f]
            if f == 0:
                pool.wait_ge(zero_filled, 16 * (NE_T // 8))
            with pool.Fori(0, NT // RING) as k:
                for r in range(RING):
                    pool.wait_ge(s["rows_ready"], k * RING + r + 1)
                    pool.sem_inc(pool_turn, 1)
                    for j in range(TOPK):
                        nc.gpsimd.indirect_dma_start(grouped_in, bass.IndirectOffsetOnAxis(idx[r][j][:, :], 0),
                                                     row_out[r][:, :], None).then_inc(s["scattered"][r], 16)
            for r in range(RING):
                pool.wait_ge(s["ye_stored"][r], 16 * NK)
            with pool.Fori(0, NT // RING) as k:
                for r in range(RING):
                    pool.wait_ge(s["idx_ready"], k * RING + r + 1)
                    pool.sem_inc(pool_turn, 1)
                    for j in range(TOPK):
                        nc.gpsimd.indirect_dma_start(got[r][j], None, grouped_out,
                                                     bass.IndirectOffsetOnAxis(idx[r][j][:, :], 0)).then_inc(s["gathered"][r], 16)

        @block.gpsimd
        def _(pool):
            nc.gpsimd.memset(zeros[:, :], 0.0).then_inc(zero_set, 1)
            nc.gpsimd.memset(ident[:, :], 0.0).then_inc(const_step, 1)
            nc.gpsimd.memset(tri[:, :], 1.0).then_inc(const_step, 1)
            nc.gpsimd.memset(seg[:, :, :], 1.0).then_inc(const_step, 1)
            pool.wait_ge(const_step, 3)
            nc.gpsimd.affine_select(out=ident[:, :], in_=ident[:, :], compare_op=ALU.not_equal, fill=1.0,
                                    base=0, pattern=[[-1, P]], channel_multiplier=1).then_inc(consts, 1)
            nc.gpsimd.affine_select(out=tri[:, :], in_=tri[:, :], compare_op=ALU.is_gt, fill=0.0,
                                    base=0, pattern=[[1, P]], channel_multiplier=-1).then_inc(consts, 1)
            nc.gpsimd.memset(seg[:, :, 0:1], 0.0).then_inc(consts, 1)
            nc.gpsimd.memset(ones[:, :], 1.0).then_inc(consts, 1)
            nc.gpsimd.memset(one_e[:, :], 1.0).then_inc(consts, 1)
            nc.gpsimd.iota(rev[:, :], [[-1, E]], base=E, channel_multiplier=0,
                           allow_small_or_imprecise_dtypes=True).then_inc(consts, 1)
            nc.gpsimd.iota(thr[:, :], [[P, NT]], base=0, channel_multiplier=0,
                           allow_small_or_imprecise_dtypes=True).then_inc(consts, 1)
            nc.gpsimd.iota(tile_no[:, :], [[1, NE_T]], base=0, channel_multiplier=0,
                           allow_small_or_imprecise_dtypes=True).then_inc(consts, 1)
            nc.gpsimd.memset(ident_b[:, :], 0.0).then_inc(const_step, 1)
            nc.gpsimd.memset(future[:, :, :], 0.0).then_inc(const_step, 1)
            nc.gpsimd.memset(head_sel[:, :, :], 0.0).then_inc(const_step, 1)
            nc.gpsimd.memset(nmax[:, :, :], 0.0).then_inc(att_consts, 1)
            for i in range(2):
                nc.gpsimd.memset(v_sb[i][:, :, :, :], 0.0).then_inc(const_step, 1)
            pool.wait_ge(const_step, 8)
            nc.gpsimd.affine_select(out=ident_b[:, :], in_=ident_b[:, :], compare_op=ALU.not_equal, fill=1.0,
                                    base=0, pattern=[[-1, P]], channel_multiplier=1).then_inc(att_consts, 1)
            nc.gpsimd.affine_select(out=future[:, :, :], in_=future[:, :, :], compare_op=ALU.is_ge, fill=NEG,
                                    base=0, pattern=[[0, 4], [-1, P]], channel_multiplier=1).then_inc(att_consts, 1)
            for part in range(3):
                nc.gpsimd.affine_select(out=head_sel[:, :, :], in_=head_sel[:, :, :], compare_op=ALU.not_equal, fill=1.0,
                                        base=-part * HEADS, pattern=[[-1, HEADS], [0, P]], channel_multiplier=1)\
                    .then_inc(const_step, 1)
                pool.wait_ge(const_step, 9 + part)
            for i in range(2):
                nc.gpsimd.memset(v_sb[i][:, :, :, D:D + 1], 1.0).then_inc(att_consts, 1)
            for n, st in enumerate(stages):
                if st == "ffn":
                    ffn_pool(pool, stages[:n].count("ffn"))
                else:
                    attn_pool(pool)

        def ffn_tensor(pe, f):
            s = ffn[f]
            logits = bank[2]

            def route_transpose(u, t):
                pe.wait_ge(s["xn_ready"], t + 1)
                for c in range(HC):
                    last = nc.tensor.transpose(bank[u][:, c * P:(c + 1) * P], xn[:, u, c * P:(c + 1) * P], ident[:, :])
                last.then_inc(s["xn_transposed"], 1)

            def route_logits(u, t):
                pe.wait_ge(s["xnT_ready"], t + 1)
                for c in range(HC):
                    last = nc.tensor.matmul(logits[:, bass.ds(t * E, E)], xnT[:, u, c, :], gwT[:, c, :],
                                            start=(c == 0), stop=(c == HC - 1))
                last.then_inc(s["logits_done"], 1)

            with pe.Fori(0, NT // 2) as k:
                for u in range(2):
                    route_transpose(u, k * 2 + u)
                    route_logits(u, k * 2 + u)
            pe.wait_ge(s["picks_ready"], 1)
            picks_v = picks[:, :, :].rearrange("p t e -> p (t e)")
            nc.tensor.matmul(bank[3][:, :], tri[:, :], picks_v, start=True, stop=True)
            nc.tensor.matmul(bank[4][:, :], ones[:, :], picks_v, start=True, stop=True).then_inc(s["counts_done"], 1)

            def transpose_in(r, k, loaded):
                u = r % 2
                j = k * RING + r
                pe.wait_ge(s["xe_loaded"][r], 16 * loaded)
                for c in range(HC):
                    last = nc.tensor.transpose(bank[u][:, c * P:(c + 1) * P], xe[:, r, c * P:(c + 1) * P], ident[:, :])
                last.then_inc(s["xe_transposed"], 1)

            def gate_up_mm(r, j, e):
                u = r % 2
                pe.wait_ge(s["xeT_ready"], j + 1)
                for c in range(HC):
                    last = nc.tensor.matmul(bank[2 + u][:, 0:2 * I], xeT[:, u, c, :], wgu_sb[:, e, c, :],
                                            start=(c == 0), stop=(c == HC - 1))
                last.then_inc(s["gu_done"], 1)

            def transpose_hid(u, j):
                pe.wait_ge(s["hid_ready"], j + 1)
                nc.tensor.transpose(bank[4 + u][:, 0:P], hid[:, u, :], ident[:, :]).then_inc(s["hid_transposed"], 1)

            def down_mm(u, j, e):
                pe.wait_ge(s["hidT_ready"], j + 1)
                later(pe, s["ye_ready"], j, 1, -1)
                nc.tensor.matmul(bank[6 + u][:, 0:H], hidT[:, u, :], wd_sb[:, e, :], start=True, stop=True).then_inc(s["down_done"], 1)

            pe.wait_ge(s["eid_ready"], 1)
            if f == 0:
                pe.wait_ge(wgu_loaded, 16 * HC * (E // 4))
                pe.wait_ge(wd_loaded, 16 * (E // 4))

            expert = [pe.alloc_register(f"expert{r}_f{f}") for r in range(RING)]

            def read_expert(j, r):
                pe.reg_load(expert[r], eid[0:1, bass.ds(j, 1)])

            def expert_of(r):
                return pe.snap(expert[r % RING], min_val=0, max_val=E - 1)

            def steps(k, rs):
                for r in rs:
                    j = k * RING + r
                    if exists(j + 1):
                        transpose_in((r + 1) % RING, k + (r + 1) // RING, k + (r + 1) // RING + 1)
                    if exists(j):
                        gate_up_mm(r, j, expert_of(r))
                    if exists(j + 1):
                        read_expert(j + 1, (r + 1) % RING)
                    if exists(j - 1):
                        transpose_hid((r - 1) % 2, j - 1)
                    if exists(j - 2):
                        down_mm(r % 2, j - 2, expert_of(r - 2))

            transpose_in(0, 0, 1)
            read_expert(0, 0)
            steps(0, range(RING))
            with pe.Fori(1, NK - 1) as k:
                steps(k, range(RING))
            steps(NK - 1, range(RING + 2))

        @block.tensor
        def _(pe):
            pe.wait_ge(consts, 8)
            pe.wait_ge(gw_loaded, 16)
            for c in range(HC):
                last = nc.tensor.transpose(bank[7][:, c * E:(c + 1) * E], gw_sb[:, c * P:(c + 1) * P], ident[0:E, 0:E])
            last.then_inc(gwT_made, 1)
            pe.wait_ge(gwT_ready, 1)
            for n, st in enumerate(stages):
                if st == "ffn":
                    ffn_tensor(pe, stages[:n].count("ffn"))
                else:
                    attn_tensor(pe)

        def ffn_scalar(act, f):
            s = ffn[f]
            act.wait_ge(s["var_ready"], 1)
            nc.scalar.activation(std[:, :], var[:, :], ACT.Sqrt).then_inc(s["std_ready"], 1)
            with act.Fori(0, NT // 2) as k:
                for u in range(2):
                    act.wait_ge(s["xn_transposed"], k * 2 + u + 1)
                    nc.scalar.copy(xnT[:, u, :, :].rearrange("p c n -> p (c n)"), bank[u][:, 0:H]).then_inc(s["xnT_ready"], 1)
            act.wait_ge(s["logits_done"], NT)
            nc.scalar.activation(prob[:, :, :].rearrange("p t e -> p (t e)"), bank[2][:, :], ACT.Sigmoid).then_inc(s["prob_ready"], 1)

            def evac_in(u, j):
                act.wait_ge(s["xe_transposed"], j + 1)
                nc.scalar.copy(xeT[:, u, :, :].rearrange("p c n -> p (c n)"), bank[u][:, 0:H]).then_inc(s["xeT_ready"], 1)

            def silu_gate(u, j):
                act.wait_ge(s["gu_done"], j + 1)
                nc.scalar.activation(silu[:, u, :], bank[2 + u][:, 0:I], ACT.Silu).then_inc(s["silu_ready"], 1)

            nc.scalar.preload_act_table(ACT.Silu)
            evac_in(0, 0)
            with act.Fori(0, NK - 1) as k:
                for r in range(RING):
                    evac_in((r + 1) % 2, k * RING + r + 1)
                    silu_gate(r % 2, k * RING + r)
            for r in range(RING):
                if r < RING - 1:
                    evac_in((r + 1) % 2, (NK - 1) * RING + r + 1)
                silu_gate(r % 2, (NK - 1) * RING + r)

        @block.scalar
        def _(act):
            act.dma_start(gw_sb[:, :], gate_w).then_inc(gw_loaded, 16)
            act.wait_ge(zero_set, 1)
            gz = grouped_in.rearrange("(n p r) h -> n p (r h)", p=P, r=8)
            for n in range(NE_T // 8):
                act.dma_start(gz[n], zeros[:, :]).then_inc(zero_filled, 16)
            for n, st in enumerate(stages):
                if st == "ffn":
                    ffn_scalar(act, stages[:n].count("ffn"))
                else:
                    attn_scalar(act)

        def row_stats(t):
            return nc.vector.bn_stats(stats[:, t, :], x_sb[:, t, :])

        def layernorm_scale(dve, s):
            nc.vector.memset(mix[0:1, 0:1], 0.0).then_inc(all_stats, 1)
            waited[0] += 1
            dve.wait_ge(all_stats, waited[0])
            nc.vector.tensor_tensor(msum[:, :], stats[:, :, 1], stats[:, :, 4], ALU.add)
            nc.vector.tensor_tensor(mdif[:, :], stats[:, :, 1], stats[:, :, 4], ALU.subtract)
            link(dve, nc.vector.tensor_tensor(vsum[:, :], stats[:, :, 2], stats[:, :, 5], ALU.add))
            nc.vector.tensor_scalar(mean[:, :], msum[:, :], 0.5, None, ALU.mult)
            link(dve, nc.vector.scalar_tensor_tensor(out=mdif[:, :], in0=mdif[:, :], scalar=0.25, in1=mdif[:, :],
                                                     op0=ALU.mult, op1=ALU.mult))
            link(dve, nc.vector.scalar_tensor_tensor(out=vsum[:, :], in0=vsum[:, :], scalar=1.0 / H, in1=mdif[:, :],
                                                     op0=ALU.mult, op1=ALU.add))
            nc.vector.tensor_scalar(var[:, :], vsum[:, :], EPS, None, ALU.add).then_inc(s["var_ready"], 1)
            dve.wait_ge(s["std_ready"], 1)
            nc.vector.reciprocal(rstd[:, :], std[:, :]).then_inc(s["rstd_ready"], 1)
            dve.wait_ge(s["rstd_ready"], 1)

        def normalise(dst, t):
            return nc.vector.tensor_scalar(dst, x_sb[:, t, :], mean[:, bass.ds(t, 1)], rstd[:, bass.ds(t, 1)],
                                           ALU.subtract, ALU.mult)

        def flat(a):
            return a[:, :, :].rearrange("p a b -> p (a b)")

        def over_e(v):
            return v[:, :].unsqueeze(2).broadcast_to([P, NT, E])

        def ffn_vector(dve, f):
            s = ffn[f]
            if f == 0:
                for c in range(LOADS):
                    dve.wait_ge(x_loaded[c], 16)
                    with dve.Fori(c * NT // LOADS, (c + 1) * NT // LOADS) as t:
                        row_stats(t).then_inc(s["stats_done"], 1)
                dve.wait_ge(s["stats_done"], NT)
            layernorm_scale(dve, s)
            for u in range(2):
                normalise(xn[:, u, :], u).then_inc(s["xn_ready"], 1)
            with dve.Fori(1, NT // 2) as k:
                for u in range(2):
                    dve.wait_ge(s["xn_transposed"], k * 2 + u - 1)
                    normalise(xn[:, u, :], k * 2 + u).then_inc(s["xn_ready"], 1)

            dve.wait_ge(s["prob_ready"], 1)
            src = prob
            for j in range(TOPK):
                link(dve, nc.vector.tensor_reduce(top[j][:, :], src[:, :, :], AX.X, ALU.max))
                link(dve, nc.vector.tensor_tensor(eq[:, :, :], src[:, :, :], over_e(top[j]), ALU.is_equal))
                link(dve, nc.vector.tensor_tensor(cand[:, :, :], eq[:, :, :],
                                                  rev[:, :].unsqueeze(1).broadcast_to([P, NT, E]), ALU.mult))
                link(dve, nc.vector.tensor_reduce(first[:, :], cand[:, :, :], AX.X, ALU.max))
                link(dve, nc.vector.tensor_tensor(pick[j][:, :, :], cand[:, :, :], over_e(first), ALU.is_equal))
                if j == 0:
                    link(dve, nc.vector.scalar_tensor_tensor(out=flat(rest), in0=flat(pick[0]), scalar=-2.0, in1=flat(prob),
                                                             op0=ALU.mult, op1=ALU.add))
                    src = rest
            nc.vector.tensor_tensor(picks[:, :, :], pick[0][:, :, :], pick[1][:, :, :], ALU.add).then_inc(s["picks_ready"], 1)
            link(dve, nc.vector.tensor_tensor(wsum[:, :], top[0][:, :], top[1][:, :], ALU.add))
            link(dve, nc.vector.reciprocal(wrec[:, :], wsum[:, :]))
            for j in range(TOPK):
                nc.vector.scalar_tensor_tensor(out=weight[:, :, j], in0=top[j][:, :], scalar=0.5, in1=wrec[:, :],
                                               op0=ALU.mult, op1=ALU.mult)
            dve.wait_ge(s["counts_done"], 1)
            link(dve, nc.vector.tensor_copy(tot[:, :, :], bank[4][:, :].rearrange("p (t e) -> p e t", e=E)))
            link(dve, nc.vector.tensor_tensor_scan(flat(cum), flat(seg), flat(tot), 0.0, ALU.mult, ALU.add))
            link(dve, nc.vector.tensor_tensor(more[:, :, :], cum[:, :, NT - 1:NT].broadcast_to([P, E, NT]),
                                              thr[:, :].unsqueeze(1).broadcast_to([P, E, NT]), ALU.is_gt))
            link(dve, nc.vector.tensor_reduce(ntile[:, :], more[:, :, :], AX.X, ALU.add))
            link(dve, nc.vector.tensor_tensor_scan(end[:, :], one_e[:, :], ntile[:, :], 0.0, ALU.mult, ALU.add))
            nc.vector.tensor_tensor(past[:, :, :], tile_no[:, :].unsqueeze(2).broadcast_to([1, NE_T, E]),
                                    end[0:1, :].unsqueeze(1).broadcast_to([1, NE_T, E]), ALU.is_ge)
            link(dve, nc.vector.tensor_tensor(begin[:, :], end[:, :], ntile[:, :], ALU.subtract))
            link(dve, nc.vector.tensor_reduce(eid_f[:, :], past[:, :, :], AX.X, ALU.add))
            nc.vector.tensor_scalar(eid[:, :], eid_f[:, :], float(E - 1), None, ALU.min).then_inc(s["eid_ready"], 1)
            link(dve, nc.vector.tensor_tensor(slot_e[:, :, :], cum[:, :, :], tot[:, :, :], ALU.subtract))
            link(dve, nc.vector.tensor_scalar(begin[:, :], begin[:, :], float(P), None, ALU.mult))
            link(dve, nc.vector.tensor_tensor(slot_e[:, :, :], slot_e[:, :, :],
                                              begin[:, :].unsqueeze(2).broadcast_to([P, E, NT]), ALU.add))
            link(dve, nc.vector.tensor_tensor(slot_t[:, :, :], bank[3][:, :].rearrange("p (t e) -> p t e", e=E),
                                              slot_e[:, :, :].rearrange("p e t -> p t e"), ALU.add))
            for j in range(TOPK):
                link(dve, nc.vector.tensor_tensor(cand[:, :, :], slot_t[:, :, :], pick[j][:, :, :], ALU.mult))
                link(dve, nc.vector.tensor_reduce(slot_f[:, :, j], cand[:, :, :], AX.X, ALU.add))
            link(dve, nc.vector.tensor_copy(slot[:, :, :], slot_f[:, :, :]))

            def dispatch(r, t, k):
                for j in range(TOPK):
                    nc.vector.tensor_copy(idx[r][j][:, :], slot[:, t, j:j + 1])
                normalise(row_out[r][:, :], t).then_inc(s["rows_ready"], 1)

            for r in range(RING):
                dispatch(r, r, 0)
            with dve.Fori(1, NT // RING) as k:
                for r in range(RING):
                    dve.wait_ge(s["scattered"][r], k * (16 * TOPK))
                    dispatch(r, k * RING + r, k)

            def gated(u, j):
                dve.wait_ge(s["silu_ready"], j + 1)
                nc.vector.tensor_tensor(hid[:, u, :], bank[2 + u][:, I:2 * I], silu[:, u, :], ALU.mult).then_inc(s["hid_ready"], 1)

            def evac_hid(u, j):
                dve.wait_ge(s["hid_transposed"], j + 1)
                nc.vector.tensor_copy(hidT[:, u, :], bank[4 + u][:, 0:P]).then_inc(s["hidT_ready"], 1)

            def evac_out(r, j, k):
                dve.wait_ge(s["down_done"], j + 1)
                later(dve, s["ye_stored"][r], k, 16, 0)
                nc.vector.tensor_copy(ye[:, r, :], bank[6 + r % 2][:, 0:H]).then_inc(s["ye_ready"], 1)

            def expert_round(k, rs):
                for r in rs:
                    j = k * RING + r
                    if exists(j - 1):
                        evac_hid((r - 1) % 2, j - 1)
                    if exists(j):
                        gated(r % 2, j)
                    if exists(j - 2):
                        evac_out((r - 2) % RING, j - 2, k - 1 if r < 2 else k)

            expert_round(0, range(RING))
            expert_round(1, range(RING))
            with dve.Fori(2, NK - 1) as k:
                expert_round(k, range(RING))
            expert_round(NK - 1, range(RING + 2))

            def fetch(r, t):
                nc.vector.tensor_copy(idx[r][0][:, :], slot[:, t, 0:1])
                nc.vector.tensor_copy(idx[r][1][:, :], slot[:, t, 1:2]).then_inc(s["idx_ready"], 1)

            def combine(r, t, k):
                dve.wait_ge(s["gathered"][r], (k + 1) * (16 * TOPK))
                nc.vector.scalar_tensor_tensor(out=mix[:, :], in0=got[r][0][:, :], scalar=weight[:, t, 0:1],
                                               in1=x_sb[:, t, :], op0=ALU.mult, op1=ALU.add).then_inc(s["mix_ready"], 1)
                dve.wait_ge(s["mix_ready"], t + 1)
                nc.vector.scalar_tensor_tensor(out=x_sb[:, t, :], in0=got[r][1][:, :], scalar=weight[:, t, 1:2],
                                               in1=mix[:, :], op0=ALU.mult, op1=ALU.add).then_inc(s["x_done"], 1)
                dve.wait_ge(s["x_done"], t + 1)
                if f < NF - 1:
                    row_stats(t)

            for r in range(RING):
                dve.wait_ge(s["scattered"][r], 16 * TOPK * NT // RING)
                fetch(r, r)
            with dve.Fori(0, NT // RING - 1) as k:
                for r in range(RING):
                    combine(r, k * RING + r, k)
                    fetch(r, k * RING + RING + r)
            for r in range(RING):
                combine(r, NT - RING + r, NT // RING - 1)

        @block.vector
        def _(dve):
            dve.wait_ge(gwT_made, 1)
            nc.vector.tensor_copy(gwT[:, :, :].rearrange("p c e -> p (c e)"), bank[7][:, 0:HC * E]).then_inc(gwT_ready, 1)
            dve.wait_ge(consts, 8)
            dve.wait_ge(wqkv_loaded, 16)
            nc.vector.tensor_scalar(wqkv_sb[:, :, 0:H], wqkv_sb[:, :, 0:H], 1.0 / float(D) ** 0.5, None, ALU.mult)\
                .then_inc(wqkv_scaled, 1)
            for n, st in enumerate(stages):
                if st == "ffn":
                    ffn_vector(dve, stages[:n].count("ffn"))
                else:
                    attn_vector(dve)


_INS = ["L0_attn_x", "L0_attn_w_qkv", "L0_attn_w_out", "L0_ffn_gate_w", "L0_ffn_gate_up_proj", "L0_ffn_down_proj"]


def kernel(**inputs):
    import numpy as _np
    import concourse.bacc as _bacc
    from concourse.bass_utils import run_bass_kernel_spmd as _run

    nc = _bacc.Bacc("TRN2", target_bir_lowering=False, num_devices=1)
    arrays, args = {}, []
    for name in _INS:
        a = _np.ascontiguousarray(inputs[name])
        arrays[f"in_{name}_dram"] = a
        args.append(nc.dram_tensor(f"in_{name}_dram", a.shape, mybir.dt.from_np(a.dtype), kind="ExternalInput").ap())
    shape = arrays["in_L0_attn_x_dram"].shape
    args.append(nc.dram_tensor("out_0_dram", shape, F32, kind="ExternalOutput").ap())
    macaron_block(nc, *args)
    r = _run(nc, [arrays], core_ids=[0])
    return r.results[0]["out_0_dram"]
```

```python
import concourse.bass as bass
from concourse import mybir
from contextlib import ExitStack

F32 = mybir.dt.float32
BF16 = mybir.dt.bfloat16
F16 = mybir.dt.float16
U32 = mybir.dt.uint32
I32 = mybir.dt.int32
ALU = mybir.AluOpType
ACT = mybir.ActivationFunctionType
AX = mybir.AxisListType

P = 128


def macaron_block(nc, x_in, w_qkv, w_out, gate_w, gate_up, down, out, stages=("ffn", "attn", "ffn")):
    B, S, H = x_in.shape
    NT = B * S // P
    HC = H // P
    E = gate_w.shape[0]
    I = down.shape[1]
    TOPK = 2
    EW = 32
    NE_T = B * S * TOPK // P + E
    RING = 4
    NK = NE_T // RING
    LOADS = 4
    PLACES = 8
    EPS = 1e-5
    HEADS, D = 16, H // 16
    NEG = -1e30
    SLOTS = 7
    VW = 32
    G = HEADS // 4
    NF = stages.count("ffn")

    x_tiles = x_in.rearrange("b (n p) h -> p (b n) h", p=P)
    out_tiles = out.rearrange("b (n p) h -> p (b n) h", p=P)

    normed = nc.dram_tensor("normed", [NT * P, H], F32).ap()
    grouped_out = nc.dram_tensor("grouped_out", [NE_T * P, H], F32).ap()

    ctx = ExitStack()
    with ctx:
        def sb(name, shape, dt=F32):
            return ctx.enter_context(nc.sbuf_tensor(name, shape, dt))

        def sem(name):
            return ctx.enter_context(nc.semaphore(name))

        bank = [ctx.enter_context(nc.psum_tensor(f"bank{i}", [P, 512], F32)) for i in range(8)]

        shared = sb("shared", [P, 4 * HEADS * S // 2])
        taken = [0]

        def lay(n, dims, **sizes):
            taken[0] += n
            assert taken[0] <= 4 * HEADS * S // 2
            return shared[:, taken[0] - n:taken[0]].rearrange(dims, **sizes)

        x_sb = sb("x_sb", [P, NT, H])
        wgu_sb = sb("wgu_sb", [P, E, HC, 2 * I])
        wd_sb = sb("wd_sb", [P, E, H])
        gw_sb = sb("gw_sb", [E, H])
        gwT = sb("gwT", [P, HC, EW])
        ident = sb("ident", [P, P])
        tri = sb("tri", [P, P], BF16)
        ones = sb("ones", [P, P], BF16)
        rev = sb("rev", [P, E])
        thr = sb("thr", [P, NT])
        tile_no = sb("tile_no", [P, NE_T])
        lane = sb("lane", [P, P])
        lane_h = sb("lane_h", [P, P], F16)
        tile_h = sb("tile_h", [P, NE_T], F16)
        token = sb("token", [P, NT])
        minus_half = sb("minus_half", [P, NT // LOADS])
        one_e = sb("one_e", [P, E])
        seg = sb("seg", [P, E, NT])
        stats = sb("stats", [P, NT, 6])
        msum = sb("msum", [P, NT])
        mdif = sb("mdif", [P, NT])
        vsum = sb("vsum", [P, NT])
        mean = sb("mean", [P, NT])
        var = sb("var", [P, NT])
        rstd = sb("rstd", [P, NT])
        xnT = shared[:, NT * E:NT * E + 2 * RING * HC * P].rearrange("p (i r c n) -> p i r c n", i=2, r=RING, c=HC)
        logitsT = sb("logitsT", [P, 2, P])
        rows = shared[:, 5 * NT * E:5 * NT * E + 2 * RING * H].rearrange("p (i r h) -> p i r h", i=2, r=RING)
        prob = lay(NT * E, "p (t e) -> p t e", e=E)
        top = [sb(f"top{k}", [P, NT]) for k in range(TOPK)]
        eq = lay(NT * E, "p (t e) -> p t e", e=E)
        cand = lay(NT * E, "p (t e) -> p t e", e=E)
        first = sb("first", [P, NT])
        pick = [lay(NT * E, "p (t e) -> p t e", e=E) for k in range(TOPK)]
        rest = lay(NT * E, "p (t e) -> p t e", e=E)
        picks = sb("picks", [P, NT, E], BF16)
        wsum = sb("wsum", [P, NT])
        wrec = sb("wrec", [P, NT])
        weight = sb("weight", [P, NT, TOPK])
        tot = lay(E * NT, "p (e t) -> p e t", e=E)
        cum = lay(E * NT, "p (e t) -> p e t", e=E)
        more = lay(E * NT, "p (e t) -> p e t", e=E)
        ntile = sb("ntile", [P, E])
        end = sb("end", [P, E])
        begin = sb("begin", [P, E])
        slot_e = more
        slot_t = lay(NT * E, "p (t e) -> p t e", e=E)
        slot_f = sb("slot_f", [P, NT, TOPK])
        slot = sb("slot", [P, NT, TOPK], U32)
        part_u = sb("part_u", [P, NT, TOPK], U32)
        tile_u = sb("tile_u", [P, NT, TOPK], U32)
        part_of = sb("part_of", [P, NT, TOPK])
        tile_of = sb("tile_of", [P, NT, TOPK])
        minus_part = sb("minus_part", [P, NT])
        is_part = lay(PLACES * P // 2, "p (r n) -> p r n", r=PLACES).bitcast(F16)
        is_tile = lay(PLACES * NE_T // 2, "p (r n) -> p r n", r=PLACES).bitcast(F16)
        source = sb("source", [P, NE_T], U32)
        distance = lay(PLACES // TOPK * P // 2, "p (r n) -> p r n", r=PLACES // TOPK).bitcast(F16)
        past = sb("past", [NE_T, E])
        passed = sb("passed", [NE_T, 1])
        place = sb("place", [P, 1])
        eid = sb("eid", [1, NE_T], I32)
        wqkv_sb = sb("wqkv_sb", [P, HC, 3 * H])
        wout_sb = sb("wout_sb", [P, HC, H])
        ident_b = sb("ident_b", [P, P], BF16)
        future = sb("future", [P, 4, P], BF16)
        head_sel = sb("head_sel", [P, HEADS, P], BF16)
        an = sb("an", [P, 2, H])
        anT = sb("anT", [P, HC, S])
        stack = [sb(f"stack{u}", [P, 2, HEADS, SLOTS, D], BF16) for u in range(2)]
        left = [sb(f"left{u}", [P, 2, HEADS, D]) for u in range(2)]
        half = HEADS * S // 2
        qT, kT = ([shared[0:SLOTS * D, (2 * a + i) * half:(2 * a + i + 1) * half].bitcast(BF16)
                   .rearrange("p (h n) -> p h n", h=HEADS) for i in range(2)] for a in range(2))
        v_sb = [sb(f"v_sb{i}", [P, 2, HEADS, VW]) for i in range(2)]
        mx = sb("mx", [P, 2, HEADS])
        nleft = sb("nleft", [P, 2, HEADS])
        nmax = sb("nmax", [P, 2, P], BF16)
        nmaxT = [sb(f"nmaxT{i}", [P, S], BF16) for i in range(2)]
        pr0 = [sb(f"pr0_{i}", [P, 4, S]) for i in range(2)]
        pr1 = [sb(f"pr1_{i}", [P, 4, P]) for i in range(2)]
        oT = sb("oT", [P, HEADS // 4, S])
        rsum = sb("rsum", [P, 2, HEADS])
        att = sb("att", [P, 2, H])
        attT = sb("attT", [P, 2, HC, P])
        idx = [[sb(f"idx{r}_{k}", [P, 1], U32) for k in range(TOPK)] for r in range(RING)]
        gathered_rows = sb("gathered_rows", [P, RING, TOPK, H])
        got = [[gathered_rows[:, r, k, :] for k in range(TOPK)] for r in range(RING)]
        xe = lay(RING * H, "p (r h) -> p r h", r=RING)
        xeT = sb("xeT", [P, 2, HC, P])
        silu = sb("silu", [P, 2, I])
        hid = sb("hid", [P, 2, I])
        hidT = sb("hidT", [P, 2, P])
        ye = shared[:, 0:RING * H].rearrange("p (r h) -> p r h", r=RING)
        mix = sb("mix", [P, 2, H])

        x_loaded = [sem(f"x_loaded{c}") for c in range(LOADS)]
        gw_loaded = sem("gw_loaded")
        wgu_loaded = sem("wgu_loaded")
        wd_loaded = sem("wd_loaded")
        consts = sem("consts")
        const_step = sem("const_step")
        gwT_made = sem("gwT_made")
        gwT_ready = sem("gwT_ready")
        halves_ready = sem("halves_ready")
        step = sem("step")
        stored = sem("stored")
        act_turn = sem("act_turn")
        pool_turn = sem("pool_turn")

        def ffn_sems(f):
            names = ["ln_step", "var_ready", "rstd_ready", "xn_ready", "xn_transposed", "xnT_ready", "logitsT_done",
                     "logitsT_ready", "logits_done", "prob_ready", "picks_ready", "counts_done", "passed_ready",
                     "passed_transposed", "eid_ready", "onehot_ready", "minus_part_ready", "distance_ready",
                     "second_ready", "source_done", "source_ready", "source_copied", "xe_transposed", "xeT_ready",
                     "gu_done", "silu_ready", "hid_ready", "hid_transposed", "hidT_ready", "down_done", "ye_ready"]
            names += ["stats_done"] if f == 0 else []
            names += ["idx_ready", "mix_ready", "x_done"] if f == NF - 1 else []
            rings = {"xn_stored": 2, "xe_loaded": RING, "ye_stored": RING, "gathered": RING if f == NF - 1 else 0}
            found = {n: sem(f"{n}_f{f}") for n in names}
            found.update({n: [sem(f"{n}{r}_f{f}") for r in range(many)] for n, many in rings.items()})
            return found

        at = {n: sem(f"{n}_at") for n in (
            "ln_step", "var_ready", "rstd_ready", "mix_ready", "mixed", "slot_copied", "gathered0", "gathered1",
            "gathered2", "gathered3", "an_ready", "an_transposed", "anT_ready", "qk_done", "hi_ready", "left_ready",
            "mid_ready", "low_ready", "parts_copied", "highs_copied", "v_done", "v_ready", "fill_done", "fill_act",
            "fill_dve", "score_done", "max_ready", "nmax_step", "nmax_ready", "nmax_transposed", "nmaxT_ready",
            "scoreT_done", "exp_ready", "masked", "pv_done", "oT_ready", "o_transposed", "rsum_ready", "att_ready",
            "att_transposed", "attT_ready", "proj_done", "x_done")}
        wqkv_loaded = sem("wqkv_loaded")
        wqkv_scaled = sem("wqkv_scaled")
        wout_loaded = sem("wout_loaded")
        att_consts = sem("att_consts")
        ffn = [ffn_sems(f) for f in range(NF)]
        count = [0]

        def link(dve, ins):
            count[0] += 1
            ins.then_inc(step, 1)
            dve.wait_ge(step, count[0])

        def later(eng, s, b, per, n):
            if isinstance(b, int) and per * b + n <= 0:
                return
            eng.wait_ge(s, b * per + n)

        def exists(j):
            return not isinstance(j, int) or 0 <= j < NE_T

        block = ctx.enter_context(nc.Block())

        SLOTS_OF, FETCH, MIX, ROOT, NORM = "slots", "fetch", "mix", "root", "norm"
        F, LOW, FILL, SCORE = "front", "low", "fill", "score"
        T, PV, UN, TR, PR = "scoreT", "pv", "untranspose", "transpose", "project"
        PE_TURN = [(0, (FILL, 0)), (-1, (F, "max")), (0, (FILL, 1)), (0, (FILL, 2)), (0, (FILL, 3)), (-1, (T, 0)),
                   (-1, (T, 1)), (-1, (T, 2)), (0, (FILL, 4)), (-1, (T, 3)), (0, (SCORE, 0)), (-1, (T, 4)),
                   (0, (FILL, 5)), (-1, (T, 5)), (0, (SCORE, 1)), (0, (FILL, 6)), (0, (SCORE, 2)), (-1, (PV, 0)),
                   (-1, (T, 6)), (-1, (T, 7)), (-1, (T, 8)), (-1, (T, 9)), (0, (SCORE, 3)), (-1, (PV, 1)),
                   (-1, (T, 10)), (0, (FILL, 7)), (-1, (T, 11)), (-1, (PV, 2)), (0, (SCORE, 4)), (1, (NORM, 0)),
                   (-1, (PV, 3)), (1, (F, "qk0")), (0, (SCORE, 5)), (0, (SCORE, 6)), (-1, (UN, 0)), (-1, (UN, 1)),
                   (1, (F, "qk1")), (0, (SCORE, 7)), (-1, (TR, 0)), (0, (SCORE, 8)), (1, (F, "v")), (0, (SCORE, 9)),
                   (0, (SCORE, 10)), (0, (SCORE, 11)), (-1, (TR, 1)), (-1, (PR, 0)), (-1, (PR, 1))]
        ACT_TURN = [(-1, (F, "max")), (0, (FILL, 2)), (-1, (T, 0)), (-1, (T, 1)), (-1, (T, 2)), (-1, (T, 3)),
                    (-1, (T, 4)), (0, (FILL, 6)), (-1, (T, 5)), (-1, (PV, 0)), (-1, (T, 6)), (-1, (T, 7)),
                    (-1, (T, 8)), (-1, (PV, 1)), (-1, (T, 9)), (-1, (T, 10)), (-1, (T, 11)), (-1, (PV, 2)),
                    (1, (NORM, 0)), (-1, (PV, 3)), (1, (F, "qk0")), (1, (F, "qk1")), (-1, (TR, 0)), (1, (F, "v")),
                    (-1, (TR, 1))]
        DVE_TURN = [(0, (FILL, 0)), (0, (FILL, 1)), (0, (FILL, 3)), (1, (MIX, 0)), (0, (SCORE, 0)), (0, (FILL, 4)),
                    (0, (SCORE, 1)), (0, (FILL, 5)), (1, (MIX, 1)), (0, (SCORE, 2)), (0, (SCORE, 3)), (0, (FILL, 7)),
                    (1, (NORM, 0)), (0, (SCORE, 4)), (1, (F, "qk0")), (0, (SCORE, 5)), (0, (SCORE, 6)),
                    (1, (LOW, 0)), (-1, (UN, 0)), (-1, (UN, 1)), (1, (F, "qk1")), (0, (SCORE, 7)), (0, (SCORE, 8)),
                    (1, (LOW, 1)), (0, (SCORE, 9)), (0, (SCORE, 10)), (0, (SCORE, 11)), (0, (F, "negate")),
                    (-1, (PR, 0)), (-1, (PR, 1))]
        POOL_TURN = [(-1, (T, 1)), (-1, (T, 2)), (2, (SLOTS_OF, 0)), (-1, (T, 4)), (2, (FETCH, 0)), (2, (FETCH, 1)),
                     (-1, (T, 5)), (-1, (T, 7)), (1, (ROOT, 0)), (-1, (T, 8)), (-1, (T, 10)), (-1, (T, 11)),
                     (2, (FETCH, 2)), (2, (FETCH, 3))]

        def batches(eng, steps, part):
            def turn(b, i):
                for after, st in steps:
                    if not isinstance(b, int) or 0 <= b + after < B:
                        part(st, b + after, (i + after) % 2)

            turn(-2, 0)
            turn(-1, 1)
            turn(0, 0)
            turn(1, 1)
            with eng.Fori(1, B // 2 - 1) as m:
                for i in range(2):
                    turn(m * 2 + i, i)
            for b in range(B - 2, B + 1):
                turn(b, b)

        bankA, bankB, bankC = bank[5], bank[6], bank[7]

        def fill_of(i):
            return i // 4, i // 2 % 2, i % 2 * 8, (bankA, bankB)[i % 2]

        FILL_ACT = (2, 6)

        def wait_fills(eng, b, n):
            later(eng, at["fill_act"], b, 2, sum(i < n for i in FILL_ACT))
            later(eng, at["fill_dve"], b, 6, sum(i not in FILL_ACT for i in range(n)))

        def score_of(n):
            return (0, 4 * n, 4) if n < G else (1, 2 * (n - G), 2)

        def scoreT_of(n):
            g, i = n // 3, n % 3
            return (0, 4 * g + 2 * i, 2) if i < 2 else (1, 4 * g, 4)

        def attn_pool(pool):
            def part(st, b, p):
                kind, n = st
                if kind == "slots":
                    for u in range(2):
                        for j in range(TOPK):
                            last = nc.gpsimd.tensor_copy(idx[2 * p + u][j][:, :], slot[:, b * 2 + u, j:j + 1])
                    last.then_inc(at["slot_copied"], 1)
                if kind == "fetch":
                    u, j = n // TOPK, n % TOPK
                    r = 2 * p + u
                    later(pool, at["slot_copied"], b, 1, 1)
                    if n == 0:
                        later(pool, at["mixed"], b, 2, -2)
                    pool.sem_inc(pool_turn, 1)
                    nc.gpsimd.indirect_dma_start(got[r][j], None, grouped_out, bass.IndirectOffsetOnAxis(idx[r][j][:, :], 0))\
                        .then_inc(at[f"gathered{r}"], 16)
                if kind == "root":
                    later(pool, at["var_ready"], b, 1, 1)
                    pool.sem_inc(pool_turn, 1)
                    nc.gpsimd.tensor_tensor(rstd[:, bass.ds(b * 2, 2)], var[:, bass.ds(b * 2, 2)], minus_half[:, 0:2], ALU.pow)\
                        .then_inc(at["rstd_ready"], 1)
                if kind == "scoreT" and n % 3:
                    g, second = n // 3, n % 3 == 2
                    later(pool, at["exp_ready"], b, 3 * G, n + 1)
                    pool.sem_inc(pool_turn, 1)
                    m = (pr1 if second else pr0)[g % 2][:, :, 0:P]
                    nc.gpsimd.affine_select(out=m, in_=m, compare_op=ALU.is_ge, fill=0.0, base=0,
                                            pattern=[[0, 4], [1, P]], channel_multiplier=-1).then_inc(at["masked"], 1)
            batches(pool, POOL_TURN, part)

        def attn_tensor(pe):
            pe.wait_ge(wqkv_scaled, 1)
            pe.wait_ge(wout_loaded, 16)
            pe.wait_ge(att_consts, 5)

            def qk_product(u, b, dst):
                for c in range(HC):
                    last = nc.tensor.matmul(dst[:, :], anT[:, c, u * P:(u + 1) * P], wqkv_sb[:, c, 0:2 * H],
                                            start=(c == 0), stop=(c == HC - 1))
                last.then_inc(at["qk_done"], 1)

            def part(st, b, p):
                kind, n = st
                if kind == "norm":
                    later(pe, at["an_ready"], b, 2, 2)
                    wait_fills(pe, b, 0)
                    for u in range(2):
                        for c in range(HC):
                            last = nc.tensor.transpose(bankA[:, c * S + u * P:c * S + (u + 1) * P],
                                                       an[:, u, c * P:(c + 1) * P], ident[:, :])
                    last.then_inc(at["an_transposed"], 1)
                elif st == ("front", "qk0"):
                    later(pe, at["anT_ready"], b, 1, 1)
                    wait_fills(pe, b, 0)
                    qk_product(0, b, bankB)
                elif st == ("front", "qk1"):
                    qk_product(1, b, bankA)
                elif st == ("front", "v"):
                    later(pe, at["left_ready"], b, 2, 1)
                    for u in range(2):
                        for c in range(HC):
                            last = nc.tensor.matmul(bankB[:, u * H:(u + 1) * H], anT[:, c, u * P:(u + 1) * P],
                                                    wqkv_sb[:, c, 2 * H:3 * H], start=(c == 0), stop=(c == HC - 1))
                    last.then_inc(at["v_done"], 1)
                elif kind == "fill":
                    u, qk, h0, dst = fill_of(n)
                    later(pe, at["parts_copied"], b, 2, u + 1)
                    later(pe, at["highs_copied"], b, 2, u + 1)
                    if n == 0:
                        later(pe, at["left_ready"], b, 2, 2)
                    elif n == 1:
                        later(pe, at["v_ready"], b, 1, 1)
                    else:
                        wait_fills(pe, b, n - 1)
                    for i in range(8):
                        last = nc.tensor.transpose(dst[:, :].bitcast(BF16)[0:SLOTS * D, i * P:(i + 1) * P],
                                                   stack[u][:, qk, h0 + i, :, :].rearrange("p s d -> p (s d)"), ident_b[:, :])
                    last.then_inc(at["fill_done"], 1)
                elif kind == "score":
                    u, h0, nh = score_of(n)
                    wait_fills(pe, b, 4 * (u + 1))
                    later(pe, at["max_ready"], b, 3 * G, n - 1)
                    dst, w = bank[3 + n % 2], P * (u + 1)
                    for i in range(nh):
                        nc.tensor.matmul(dst[:, i * w:(i + 1) * w], qT[p][:, h0 + i, u * P:(u + 1) * P], kT[p][:, h0 + i, 0:w],
                                         start=(i == 0), stop=False, skip_group_check=True)
                    diag = dst[:, :].rearrange("p (h k) -> p h k", k=w)[:, :, u * P:(u + 1) * P]
                    nc.tensor.matmul(diag, ident_b[:, :], future[:, 0:nh, :], start=False, stop=True,
                                     skip_group_check=True).then_inc(at["score_done"], 1)
                elif st == ("front", "max"):
                    later(pe, at["nmax_ready"], b, 1, 1)
                    later(pe, at["attT_ready"], b, 2, 0)
                    for u in range(2):
                        last = nc.tensor.transpose(bankC[:, :].bitcast(BF16)[:, u * P:(u + 1) * P], nmax[:, u, :], ident_b[:, :])
                    last.then_inc(at["nmax_transposed"], 1)
                elif kind == "scoreT":
                    kt, h0, nh = scoreT_of(n)
                    later(pe, at["nmaxT_ready"], b, 1, 1)
                    later(pe, at["exp_ready"], b, 3 * G, n - 2)
                    if n < 2:
                        later(pe, at["x_done"], b, 2, n - 1)
                    dst, w = bank[n % 3], S - kt * P
                    for i in range(nh):
                        h = h0 + i
                        nc.tensor.matmul(dst[:, i * w:(i + 1) * w], kT[p][:, h, kt * P:(kt + 1) * P], qT[p][:, h, kt * P:S],
                                         start=(i == 0), stop=False, skip_group_check=True)
                        last = nc.tensor.matmul(dst[:, i * w:(i + 1) * w], head_sel[:, h, :], nmaxT[p][:, kt * P:S],
                                                start=False, stop=True, skip_group_check=True)
                    last.then_inc(at["scoreT_done"], 1)
                elif kind == "pv":
                    later(pe, at["masked"], b, 2 * G, 2 * n + 2)
                    later(pe, at["oT_ready"], b, G, n)
                    cols = n % 2 * S
                    for kt in range(2):
                        for j in range(4):
                            rhs = pr0[n % 2][:, j, :] if kt == 0 else pr1[n % 2][:, j, :]
                            last = nc.tensor.matmul(bankC[j * VW:(j + 1) * VW, cols + kt * P:cols + S],
                                                    v_sb[p][:, kt, 4 * n + j, :], rhs, start=(kt == 0), stop=(kt == 1),
                                                    skip_group_check=True)
                    last.then_inc(at["pv_done"], 1)
                elif kind == "untranspose":
                    later(pe, at["oT_ready"], b, G, G)
                    later(pe, at["exp_ready"], b, 3 * G, 3 * G)
                    for g in range(G):
                        last = nc.tensor.transpose(bank[n][:, g * P:(g + 1) * P], oT[:, g, n * P:(n + 1) * P], ident[:, :])
                    last.then_inc(at["o_transposed"], 1)
                elif kind == "transpose":
                    later(pe, at["att_ready"], b, 2, n + 1)
                    for c in range(HC):
                        last = nc.tensor.transpose((bankC, bank[2])[n][:, c * P:(c + 1) * P], att[:, n, c * P:(c + 1) * P], ident[:, :])
                    last.then_inc(at["att_transposed"], 1)
                elif kind == "project":
                    later(pe, at["attT_ready"], b, 2, n + 1)
                    for c in range(HC):
                        last = nc.tensor.matmul(bank[n][:, 0:H], attT[:, n, c, :], wout_sb[:, c, :], start=(c == 0), stop=(c == HC - 1))
                    last.then_inc(at["proj_done"], 1)
            batches(pe, PE_TURN, part)

        def attn_scalar(act):
            def part(st, b, p):
                kind, n = st
                if kind == "norm":
                    later(act, at["an_transposed"], b, 1, 1)
                    nc.scalar.copy(anT[:, :, :].rearrange("p c n -> p (c n)"), bankA[:, :]).then_inc(at["anT_ready"], 1)
                elif kind == "front" and n in ("qk0", "qk1"):
                    u = int(n[2])
                    src = (bankB, bankA)[u]
                    later(act, at["qk_done"], b, 2, u + 1)
                    nc.scalar.copy(stack[u][:, :, :, 0, :].rearrange("p a h d -> p (a h) d"),
                                         src[:, :].rearrange("p (h d) -> p h d", d=D)).then_inc(at["hi_ready"], 1)
                    later(act, at["hi_ready"], b, 2, u + 1)
                    for qk, to in ((0, 3), (1, 5)):
                        last = nc.scalar.copy(stack[u][:, qk, :, to:to + 2, :],
                                              stack[u][:, qk, :, 0:1, :].broadcast_to([P, HEADS, 2, D]))
                    last.then_inc(at["highs_copied"], 1)
                    later(act, at["left_ready"], b, 2, u + 1)
                    nc.scalar.copy(stack[u][:, :, :, 1, :].rearrange("p a h d -> p (a h) d"),
                                         left[u][:, :, :, :].rearrange("p a h d -> p (a h) d")).then_inc(at["mid_ready"], 1)
                elif st == ("front", "v"):
                    later(act, at["v_done"], b, 1, 1)
                    nc.scalar.copy(v_sb[p][:, :, :, 0:D], bankB[:, :].rearrange("p (u h d) -> p u h d", u=2, d=D))\
                        .then_inc(at["v_ready"], 1)
                elif kind == "pv":
                    later(act, at["pv_done"], b, G, n + 1)
                    nc.scalar.copy(oT[:, n, :], bankC[:, n % 2 * S:(n % 2 + 1) * S]).then_inc(at["oT_ready"], 1)
                elif kind == "fill" and n in FILL_ACT:
                    u, qk, h0, src = fill_of(n)
                    later(act, at["fill_done"], b, 8, n + 1)
                    dst = (qT, kT)[qk][p]
                    nc.scalar.copy(dst[:, h0:h0 + 8, u * P:(u + 1) * P],
                                         src[:, :].bitcast(BF16)[0:SLOTS * D, :].rearrange("p (h n) -> p h n", n=P)).then_inc(at["fill_act"], 1)
                elif st == ("front", "max"):
                    later(act, at["nmax_transposed"], b, 1, 1)
                    nc.scalar.copy(nmaxT[p][:, :], bankC[:, :].bitcast(BF16)[:, 0:S]).then_inc(at["nmaxT_ready"], 1)
                elif kind == "scoreT":
                    kt, h0, nh = scoreT_of(n)
                    g = n // 3
                    later(act, at["scoreT_done"], b, 3 * G, n + 1)
                    if n % 3 == 0:
                        later(act, at["pv_done"], b, G, g - 1)
                    dst = pr1[g % 2][:, :, :] if kt else pr0[g % 2][:, h0 % 4:h0 % 4 + 2, :]
                    nc.scalar.activation(dst.rearrange("p h n -> p (h n)"), bank[n % 3][:, :], ACT.Exp).then_inc(at["exp_ready"], 1)
                elif kind == "transpose":
                    later(act, at["att_transposed"], b, 2, n + 1)
                    nc.scalar.copy(attT[:, n, :, :].rearrange("p c n -> p (c n)"), (bankC, bank[2])[n][:, 0:H]).then_inc(at["attT_ready"], 1)
            batches(act, ACT_TURN, part)

        def attn_vector(dve):
            dve.wait_ge(wqkv_loaded, 16)
            nc.vector.tensor_scalar(wqkv_sb[:, :, 0:H], wqkv_sb[:, :, 0:H], 1.0 / float(D) ** 0.5, None, ALU.mult)\
                .then_inc(wqkv_scaled, 1)

            def mix_in(b, p):
                for u in range(2):
                    t = b * 2 + u
                    later(dve, at[f"gathered{2 * p + u}"], b, 16, 32 - 16 * p)
                    nc.vector.scalar_tensor_tensor(out=mix[:, u, :], in0=got[2 * p + u][0], scalar=weight[:, t, 0:1],
                                                   in1=x_sb[:, t, :], op0=ALU.mult, op1=ALU.add).then_inc(at["mix_ready"], 1)
                for u in range(2):
                    t = b * 2 + u
                    later(dve, at["mix_ready"], b, 2, u + 1)
                    nc.vector.scalar_tensor_tensor(out=x_sb[:, t, :], in0=got[2 * p + u][1], scalar=weight[:, t, 1:2],
                                                   in1=mix[:, u, :], op0=ALU.mult, op1=ALU.add).then_inc(at["mixed"], 1)

            def moments_of(b, p):
                for u in range(2):
                    later(dve, at["mixed"], b, 2, u + 1)
                    last = row_stats(b * 2 + u)
                last.then_inc(at["ln_step"], 1)
                later(dve, at["ln_step"], b, 3, 1)
                ts = bass.ds(b * 2, 2)
                nc.vector.tensor_tensor(mdif[:, ts], stats[:, ts, 1], stats[:, ts, 4], ALU.subtract)
                nc.vector.scalar_tensor_tensor(out=vsum[:, ts], in0=stats[:, ts, 2], scalar=EPS * H, in1=stats[:, ts, 5],
                                               op0=ALU.add, op1=ALU.add)
                nc.vector.tensor_tensor(msum[:, ts], stats[:, ts, 1], stats[:, ts, 4], ALU.add).then_inc(at["ln_step"], 1)
                later(dve, at["ln_step"], b, 3, 2)
                nc.vector.scalar_tensor_tensor(out=mdif[:, ts], in0=mdif[:, ts], scalar=0.25, in1=mdif[:, ts],
                                               op0=ALU.mult, op1=ALU.mult)
                nc.vector.tensor_scalar(mean[:, ts], msum[:, ts], 0.5, None, ALU.mult).then_inc(at["ln_step"], 1)
                later(dve, at["ln_step"], b, 3, 3)
                nc.vector.scalar_tensor_tensor(out=var[:, ts], in0=vsum[:, ts], scalar=1.0 / H, in1=mdif[:, ts],
                                               op0=ALU.mult, op1=ALU.add).then_inc(at["var_ready"], 1)

            def split(u, b):
                src = (bankB, bankA)[u]
                later(dve, at["hi_ready"], b, 2, u + 1)
                nc.vector.tensor_tensor(left[u][:, :, :, :].rearrange("p a h d -> p (a h) d"),
                                        src[:, :].rearrange("p (h d) -> p h d", d=D),
                                        stack[u][:, :, :, 0, :].rearrange("p a h d -> p (a h) d"), ALU.subtract)\
                    .then_inc(at["left_ready"], 1)

            def split_low(u, b):
                later(dve, at["mid_ready"], b, 2, u + 1)
                nc.vector.tensor_tensor(stack[u][:, :, :, 2, :].rearrange("p a h d -> p (a h) d"),
                                        left[u][:, :, :, :].rearrange("p a h d -> p (a h) d"),
                                        stack[u][:, :, :, 1, :].rearrange("p a h d -> p (a h) d"), ALU.subtract)\
                    .then_inc(at["low_ready"], 1)
                later(dve, at["low_ready"], b, 2, u + 1)
                for qk, to in ((0, 5), (1, 3)):
                    last = nc.vector.tensor_copy(stack[u][:, qk, :, to:to + 2, :], stack[u][:, qk, :, 1:3, :])
                last.then_inc(at["parts_copied"], 1)

            def part(st, b, p):
                kind, n = st
                if kind == "mix":
                    (mix_in if n == 0 else moments_of)(b, p)
                elif kind == "norm":
                    later(dve, at["rstd_ready"], b, 1, 1)
                    later(dve, at["an_transposed"], b, 1, 0)
                    for u in range(2):
                        normalise(an[:, u, :], b * 2 + u).then_inc(at["an_ready"], 1)
                elif st == ("front", "qk0"):
                    split(0, b)
                elif st == ("front", "qk1"):
                    split(1, b)
                elif kind == "low":
                    split_low(n, b)
                elif kind == "fill" and n not in FILL_ACT:
                    u, qk, h0, src = fill_of(n)
                    later(dve, at["fill_done"], b, 8, n + 1)
                    dst = (qT, kT)[qk][p]
                    nc.vector.tensor_copy(dst[:, h0:h0 + 8, u * P:(u + 1) * P],
                                          src[:, :].bitcast(BF16)[0:SLOTS * D, :].rearrange("p (h n) -> p h n", n=P))\
                        .then_inc(at["fill_dve"], 1)
                elif kind == "score":
                    u, h0, nh = score_of(n)
                    later(dve, at["score_done"], b, 3 * G, n + 1)
                    nc.vector.tensor_reduce(mx[:, u, h0:h0 + nh], bank[3 + n % 2][:, :].rearrange("p (h k) -> p h k", h=nh),
                                            AX.X, ALU.max).then_inc(at["max_ready"], 1)
                elif st == ("front", "negate"):
                    later(dve, at["max_ready"], b, 3 * G, 3 * G)
                    nc.vector.tensor_scalar(nmax[:, :, 0:HEADS], mx[:, :, :], -1.0, None, ALU.mult).then_inc(at["nmax_step"], 1)
                    later(dve, at["nmax_step"], b, 3, 1)
                    nc.vector.scalar_tensor_tensor(out=nleft[:, :, :], in0=mx[:, :, :], scalar=-1.0, in1=nmax[:, :, 0:HEADS],
                                                   op0=ALU.mult, op1=ALU.subtract).then_inc(at["nmax_step"], 1)
                    later(dve, at["nmax_step"], b, 3, 2)
                    nc.vector.tensor_copy(nmax[:, :, HEADS:2 * HEADS], nleft[:, :, :]).then_inc(at["nmax_step"], 1)
                    later(dve, at["nmax_step"], b, 3, 3)
                    nc.vector.tensor_tensor(nmax[:, :, 2 * HEADS:3 * HEADS], nleft[:, :, :], nmax[:, :, HEADS:2 * HEADS],
                                            ALU.subtract).then_inc(at["nmax_ready"], 1)
                elif kind == "untranspose":
                    later(dve, at["o_transposed"], b, 2, n + 1)
                    o = bank[n][:, :].rearrange("p (h d) -> p h d", d=VW)
                    nc.vector.reciprocal(rsum[:, n, :], o[:, :, D]).then_inc(at["rsum_ready"], 1)
                    later(dve, at["rsum_ready"], b, 2, n + 1)
                    nc.vector.tensor_tensor(att[:, n, :].rearrange("p (h d) -> p h d", d=D), o[:, :, 0:D],
                                            rsum[:, n, :].unsqueeze(2).broadcast_to([P, HEADS, D]), ALU.mult).then_inc(at["att_ready"], 1)
                elif kind == "project":
                    later(dve, at["proj_done"], b, 2, n + 1)
                    t = b * 2 + n
                    nc.vector.tensor_tensor(x_sb[:, t, :], bank[n][:, 0:H], x_sb[:, t, :], ALU.add).then_inc(at["x_done"], 1)
                    later(dve, at["x_done"], b, 2, n + 1)
                    row_stats(t)
            batches(dve, DVE_TURN, part)

        def ffn_sync(sp, f):
            s = ffn[f]

            def store_normed(i, k):
                sp.wait_ge(s["xn_ready"], (k * 2 + i + 1) * RING)
                sp.dma_start(normed.rearrange("(n p) h -> p n h", p=P)[:, bass.ds((k * 2 + i) * RING, RING), :],
                             rows[:, i, :, :]).then_inc(s["xn_stored"][i], 16)

            def store(r, k):
                sp.wait_ge(s["ye_ready"], k * RING + r + 1)
                sp.dma_start(grouped_out[bass.ds((k * RING + r) * P, P), :], ye[:, r, :]).then_inc(s["ye_stored"][r], 16)

            with sp.Fori(0, NT // RING // 2) as k:
                for i in range(2):
                    store_normed(i, k)
            if f == 0:
                for g in range(0, E, 4):
                    if g == 4:
                        sp.dma_start(wqkv_sb[:, :, :], w_qkv.rearrange("(c p) f -> p c f", p=P)).then_inc(wqkv_loaded, 16)
                        sp.dma_start(wout_sb[:, :, :], w_out.rearrange("(c p) f -> p c f", p=P)).then_inc(wout_loaded, 16)
                    for c in range(HC):
                        sp.dma_start(wgu_sb[:, g:g + 4, c, :],
                                     gate_up[g:g + 4, c * P:(c + 1) * P, :].rearrange("e p f -> p e f")).then_inc(wgu_loaded, 16)
                    sp.dma_start(wd_sb[:, g:g + 4, :], down[g:g + 4].rearrange("e i h -> i e h")).then_inc(wd_loaded, 16)
            with sp.Fori(0, NK) as k:
                for r in range(RING):
                    store(r, k)

        @block.sync
        def _(sp):
            step_ = NT // LOADS
            for c in range(LOADS):
                sp.dma_start(x_sb[:, c * step_:(c + 1) * step_, :], x_tiles[:, c * step_:(c + 1) * step_, :]).then_inc(x_loaded[c], 16)
            for n, st in enumerate(stages):
                if st == "ffn":
                    ffn_sync(sp, stages[:n].count("ffn"))
            s = ffn[NF - 1]
            with sp.Fori(0, NT // 2) as k:
                sp.wait_ge(s["x_done"], k * 2 + 2)
                sp.dma_start(out_tiles[:, bass.ds(k * 2, 2), :], x_sb[:, bass.ds(k * 2, 2), :]).then_inc(stored, 16)
            sp.wait_ge(stored, 16 * (NT // 2))

        def ffn_pool(pool, f):
            s = ffn[f]

            def inverse_root(c):
                pool.wait_ge(s["var_ready"], c + 1)
                w = NT // LOADS
                nc.gpsimd.tensor_tensor(rstd[:, c * w:(c + 1) * w], var[:, c * w:(c + 1) * w], minus_half[:, :], ALU.pow)\
                    .then_inc(s["rstd_ready"], 1)

            for c in range(LOADS):
                inverse_root(c)

            def fetch(k, r):
                j = k * RING + r
                later(pool, s["xe_transposed"], k, RING, r - RING + 1)
                pool.sem_inc(pool_turn, 1)
                nc.gpsimd.tensor_copy(idx[r][0][:, :], source[:, bass.ds(j, 1)]).then_inc(s["source_copied"], 1)
                pool.wait_ge(s["source_copied"], j + 1)
                pool.sem_inc(pool_turn, 1)
                nc.gpsimd.indirect_dma_start(xe[:, r, :], None, normed,
                                             bass.IndirectOffsetOnAxis(idx[r][0][:, :], 0)).then_inc(s["xe_loaded"][r], 16)

            pool.wait_ge(s["xn_transposed"], NT)
            for q in range(2):
                pool.wait_ge(s["xn_stored"][q], 16 * (NT // RING // 2))
            pool.wait_ge(s["source_ready"], 1)
            for r in range(RING):
                fetch(0, r)
            with pool.Fori(1, NK) as k:
                for r in range(RING):
                    fetch(k, r)
            for r in range(RING):
                pool.wait_ge(s["ye_stored"][r], 16 * NK)
            if f < NF - 1:
                return
            with pool.Fori(0, NT // RING) as k:
                for r in range(RING):
                    pool.wait_ge(s["idx_ready"], k * RING + r + 1)
                    pool.sem_inc(pool_turn, 1)
                    for j in range(TOPK):
                        nc.gpsimd.indirect_dma_start(got[r][j], None, grouped_out,
                                                     bass.IndirectOffsetOnAxis(idx[r][j][:, :], 0)).then_inc(s["gathered"][r], 16)

        @block.gpsimd
        def _(pool):
            nc.gpsimd.memset(ident[:, :], 0.0).then_inc(const_step, 1)
            nc.gpsimd.memset(tri[:, :], 1.0).then_inc(const_step, 1)
            nc.gpsimd.memset(seg[:, :, :], 1.0).then_inc(const_step, 1)
            pool.wait_ge(const_step, 3)
            nc.gpsimd.affine_select(out=ident[:, :], in_=ident[:, :], compare_op=ALU.not_equal, fill=1.0,
                                    base=0, pattern=[[-1, P]], channel_multiplier=1).then_inc(consts, 1)
            nc.gpsimd.affine_select(out=tri[:, :], in_=tri[:, :], compare_op=ALU.is_gt, fill=0.0,
                                    base=0, pattern=[[1, P]], channel_multiplier=-1).then_inc(consts, 1)
            nc.gpsimd.memset(seg[:, :, 0:1], 0.0).then_inc(consts, 1)
            nc.gpsimd.memset(ones[:, :], 1.0).then_inc(consts, 1)
            nc.gpsimd.memset(one_e[:, :], 1.0).then_inc(consts, 1)
            nc.gpsimd.iota(rev[:, :], [[-1, E]], base=E, channel_multiplier=0,
                           allow_small_or_imprecise_dtypes=True).then_inc(consts, 1)
            nc.gpsimd.iota(thr[:, :], [[P, NT]], base=0, channel_multiplier=0,
                           allow_small_or_imprecise_dtypes=True).then_inc(consts, 1)
            nc.gpsimd.iota(tile_no[:, :], [[1, NE_T]], base=0, channel_multiplier=0,
                           allow_small_or_imprecise_dtypes=True).then_inc(consts, 1)
            nc.gpsimd.iota(lane[:, :], [[1, P]], base=0, channel_multiplier=0,
                           allow_small_or_imprecise_dtypes=True).then_inc(consts, 1)
            nc.gpsimd.iota(token[:, :], [[P, NT]], base=-NT * P // 2, channel_multiplier=1,
                           allow_small_or_imprecise_dtypes=True).then_inc(consts, 1)
            nc.gpsimd.memset(minus_half[:, :], -0.5).then_inc(consts, 1)
            nc.gpsimd.iota(place[:, :], [[1, 1]], base=0, channel_multiplier=1,
                           allow_small_or_imprecise_dtypes=True).then_inc(consts, 1)
            pool.wait_ge(consts, 12)
            nc.gpsimd.memset(ident_b[:, :], 0.0).then_inc(const_step, 1)
            nc.gpsimd.memset(future[:, :, :], 0.0).then_inc(const_step, 1)
            nc.gpsimd.memset(head_sel[:, :, :], 0.0).then_inc(const_step, 1)
            nc.gpsimd.memset(nmax[:, :, :], 0.0).then_inc(att_consts, 1)
            for i in range(2):
                nc.gpsimd.memset(v_sb[i][:, :, :, :], 0.0).then_inc(const_step, 1)
            pool.wait_ge(const_step, 8)
            nc.gpsimd.affine_select(out=ident_b[:, :], in_=ident_b[:, :], compare_op=ALU.not_equal, fill=1.0,
                                    base=0, pattern=[[-1, P]], channel_multiplier=1).then_inc(att_consts, 1)
            nc.gpsimd.affine_select(out=future[:, :, :], in_=future[:, :, :], compare_op=ALU.is_ge, fill=NEG,
                                    base=0, pattern=[[0, 4], [-1, P]], channel_multiplier=1).then_inc(att_consts, 1)
            for part in range(3):
                nc.gpsimd.affine_select(out=head_sel[:, :, :], in_=head_sel[:, :, :], compare_op=ALU.not_equal, fill=1.0,
                                        base=-part * HEADS, pattern=[[-1, HEADS], [0, P]], channel_multiplier=1)\
                    .then_inc(const_step, 1)
                pool.wait_ge(const_step, 9 + part)
            for i in range(2):
                nc.gpsimd.memset(v_sb[i][:, :, :, D:D + 1], 1.0).then_inc(att_consts, 1)
            for n, st in enumerate(stages):
                if st == "ffn":
                    ffn_pool(pool, stages[:n].count("ffn"))
                else:
                    attn_pool(pool)

        def ffn_tensor(pe, f):
            s = ffn[f]

            def route_transposes(i, k):
                for r in range(RING):
                    pe.wait_ge(s["xn_ready"], k * RING + r + 1)
                    later(pe, s["xnT_ready"], k, RING, r - RING + 1)
                    for c in range(HC):
                        last = nc.tensor.transpose(bank[r][:, c * P:(c + 1) * P], rows[:, i, r, c * P:(c + 1) * P], ident[:, :])
                    last.then_inc(s["xn_transposed"], 1)

            def route_logits(i, k):
                pe.wait_ge(s["xnT_ready"], (k + 1) * RING)
                later(pe, s["logitsT_ready"], k, 1, 0)
                for c in range(HC):
                    for r in range(RING):
                        last = nc.tensor.matmul(bank[4][r * EW:(r + 1) * EW, 0:P], gwT[:, c, :], xnT[:, i, r, c, :],
                                                start=(c == 0), stop=(c == HC - 1), skip_group_check=True)
                last.then_inc(s["logitsT_done"], 1)

            ROUNDS = NT // RING
            for k in range(ROUNDS + 1):
                if k < ROUNDS:
                    route_transposes(k % 2, k)
                if k > 0:
                    q = k - 1
                    route_logits(q % 2, q)
                if k > 1 or k == ROUNDS:
                    for q in ([k - 2] if k < ROUNDS else [k - 2, k - 1]):
                        pe.wait_ge(s["logitsT_ready"], q + 1)
                        nc.tensor.transpose(bank[5 + q // 4][:, q % 4 * P:(q % 4 + 1) * P], logitsT[:, q % 2, :], ident[:, :])\
                            .then_inc(s["logits_done"], 1)
            pe.wait_ge(s["picks_ready"], 1)
            picks_v = picks[:, :, :].rearrange("p t e -> p (t e)")
            nc.tensor.matmul(bank[3][:, :], tri[:, :], picks_v, start=True, stop=True)
            nc.tensor.matmul(bank[4][:, :], ones[:, :], picks_v, start=True, stop=True).then_inc(s["counts_done"], 1)

            pe.wait_ge(s["passed_ready"], 1)
            nc.tensor.transpose(bank[6][0:1, 0:NE_T], passed[:, :], ident[0:NE_T, 0:NE_T]).then_inc(s["passed_transposed"], 1)

            def place_tokens(k, r, first, last):
                pe.wait_ge(s["onehot_ready"], k * PLACES + r + 1)
                if r % TOPK:
                    pe.wait_ge(s["second_ready"], k * (PLACES // TOPK) + r // TOPK + 1)
                nc.tensor.matmul(bank[5][:, 0:NE_T], is_part[:, r, :], is_tile[:, r, :], start=first, stop=last,
                                 skip_group_check=True).then_inc(s["source_done"], 1)

            turns = NT * TOPK // PLACES
            for r in range(PLACES):
                place_tokens(0, r, r == 0, False)
            with pe.Fori(1, turns - 1) as k:
                for r in range(PLACES):
                    place_tokens(k, r, False, False)
            for r in range(PLACES):
                place_tokens(turns - 1, r, False, r == PLACES - 1)

            def transpose_in(r, k, loaded):
                u = r % 2
                j = k * RING + r
                pe.wait_ge(s["xe_loaded"][r], 16 * loaded)
                for c in range(HC):
                    last = nc.tensor.transpose(bank[u][:, c * P:(c + 1) * P], xe[:, r, c * P:(c + 1) * P], ident[:, :])
                last.then_inc(s["xe_transposed"], 1)

            def gate_up_mm(r, j, e):
                u = r % 2
                pe.wait_ge(s["xeT_ready"], j + 1)
                for c in range(HC):
                    last = nc.tensor.matmul(bank[2 + u][:, 0:2 * I], xeT[:, u, c, :], wgu_sb[:, e, c, :],
                                            start=(c == 0), stop=(c == HC - 1))
                last.then_inc(s["gu_done"], 1)

            def transpose_hid(u, j):
                pe.wait_ge(s["hid_ready"], j + 1)
                nc.tensor.transpose(bank[4 + u][:, 0:P], hid[:, u, :], ident[:, :]).then_inc(s["hid_transposed"], 1)

            def down_mm(u, j, e):
                pe.wait_ge(s["hidT_ready"], j + 1)
                later(pe, s["ye_ready"], j, 1, -1)
                nc.tensor.matmul(bank[6 + u][:, 0:H], hidT[:, u, :], wd_sb[:, e, :], start=True, stop=True).then_inc(s["down_done"], 1)

            pe.wait_ge(s["eid_ready"], 1)
            if f == 0:
                pe.wait_ge(wgu_loaded, 16 * HC * (E // 4))
                pe.wait_ge(wd_loaded, 16 * (E // 4))

            expert = [pe.alloc_register(f"expert{r}_f{f}") for r in range(RING)]

            def read_expert(j, r):
                pe.reg_load(expert[r], eid[0:1, bass.ds(j, 1)])

            def expert_of(r):
                return pe.snap(expert[r % RING], min_val=0, max_val=E - 1)

            def steps(k, rs):
                for r in rs:
                    j = k * RING + r
                    if exists(j + 1):
                        transpose_in((r + 1) % RING, k + (r + 1) // RING, k + (r + 1) // RING + 1)
                    if exists(j):
                        gate_up_mm(r, j, expert_of(r))
                    if exists(j + 1):
                        read_expert(j + 1, (r + 1) % RING)
                    if exists(j - 1):
                        transpose_hid((r - 1) % 2, j - 1)
                    if exists(j - 2):
                        down_mm(r % 2, j - 2, expert_of(r - 2))

            transpose_in(0, 0, 1)
            read_expert(0, 0)
            steps(0, range(RING))
            with pe.Fori(1, NK - 1) as k:
                steps(k, range(RING))
            steps(NK - 1, range(RING + 2))

        @block.tensor
        def _(pe):
            pe.wait_ge(consts, 12)
            pe.wait_ge(gw_loaded, 16)
            for c in range(HC):
                last = nc.tensor.transpose(bank[7][:, c * E:(c + 1) * E], gw_sb[:, c * P:(c + 1) * P], ident[0:E, 0:E])
            last.then_inc(gwT_made, 1)
            pe.wait_ge(gwT_ready, 1)
            for n, st in enumerate(stages):
                if st == "ffn":
                    ffn_tensor(pe, stages[:n].count("ffn"))
                else:
                    attn_tensor(pe)

        def ffn_scalar(act, f):
            s = ffn[f]

            def route_copies(k, i):
                for r in range(RING):
                    act.wait_ge(s["xn_transposed"], k * RING + r + 1)
                    later(act, s["logitsT_done"], k, 1, -1)
                    nc.scalar.copy(xnT[:, i, r, :, :].rearrange("p c n -> p (c n)"), bank[r][:, 0:H]).then_inc(s["xnT_ready"], 1)

            def logits_copy(k, i):
                act.wait_ge(s["logitsT_done"], k + 1)
                later(act, s["logits_done"], k, 1, -1)
                nc.scalar.copy(logitsT[:, i, :], bank[4][:, 0:P]).then_inc(s["logitsT_ready"], 1)

            nc.scalar.preload_act_table(ACT.Sigmoid)
            for k in range(NT // RING):
                route_copies(k, k % 2)
                if k:
                    logits_copy(k - 1, (k - 1) % 2)
            logits_copy(NT // RING - 1, (NT // RING - 1) % 2)
            act.wait_ge(s["logits_done"], NT // RING)
            for i in range(2):
                last = nc.scalar.activation(prob[:, i * NT // 2:(i + 1) * NT // 2, :],
                                            bank[5 + i][:, :].rearrange("p (t w) -> p t w", w=EW)[:, :, 0:E], ACT.Sigmoid)
            last.then_inc(s["prob_ready"], 1)

            def evac_in(u, j):
                act.wait_ge(s["xe_transposed"], j + 1)
                nc.scalar.copy(xeT[:, u, :, :].rearrange("p c n -> p (c n)"), bank[u][:, 0:H]).then_inc(s["xeT_ready"], 1)

            def silu_gate(u, j):
                act.wait_ge(s["gu_done"], j + 1)
                nc.scalar.activation(silu[:, u, :], bank[2 + u][:, 0:I], ACT.Silu).then_inc(s["silu_ready"], 1)

            def second_parts(k):
                n = PLACES // TOPK
                later(act, s["second_ready"], k, n, 0)
                act.sem_inc(act_turn, 1)
                for q in range(n):
                    nc.scalar.activation(distance[:, q, :], lane_h[:, :], ACT.Abs, bias=minus_part[:, bass.ds(k * n + q, 1)])\
                        .then_inc(s["distance_ready"], 1)
                for q in range(n):
                    act.wait_ge(s["distance_ready"], k * n + q + 1)
                    later(act, s["source_done"], k, PLACES, q * TOPK + 2 - PLACES)
                    nc.scalar.activation(is_part[:, q * TOPK + 1, :], distance[:, q, :], ACT.Relu, scale=-1.0, bias=one_e[:, 0:1])\
                        .then_inc(s["second_ready"], 1)

            act.wait_ge(s["minus_part_ready"], 1)
            second_parts(0)
            with act.Fori(1, NT * TOPK // PLACES) as k:
                second_parts(k)

            nc.scalar.preload_act_table(ACT.Silu)
            evac_in(0, 0)
            with act.Fori(0, NK - 1) as k:
                for r in range(RING):
                    evac_in((r + 1) % 2, k * RING + r + 1)
                    silu_gate(r % 2, k * RING + r)
            for r in range(RING):
                if r < RING - 1:
                    evac_in((r + 1) % 2, (NK - 1) * RING + r + 1)
                silu_gate(r % 2, (NK - 1) * RING + r)

        @block.scalar
        def _(act):
            act.dma_start(gw_sb[:, :], gate_w).then_inc(gw_loaded, 16)
            for n, st in enumerate(stages):
                if st == "ffn":
                    ffn_scalar(act, stages[:n].count("ffn"))
                else:
                    attn_scalar(act)

        def row_stats(t):
            return nc.vector.bn_stats(stats[:, t, :], x_sb[:, t, :])

        def layernorm_moments(dve, s, ts, n):
            nc.vector.tensor_tensor(msum[:, ts], stats[:, ts, 1], stats[:, ts, 4], ALU.add)
            nc.vector.tensor_tensor(mdif[:, ts], stats[:, ts, 1], stats[:, ts, 4], ALU.subtract)
            nc.vector.tensor_tensor(vsum[:, ts], stats[:, ts, 2], stats[:, ts, 5], ALU.add).then_inc(s["ln_step"], 1)
            dve.wait_ge(s["ln_step"], n * 3 + 1)
            nc.vector.tensor_scalar(mean[:, ts], msum[:, ts], 0.5, None, ALU.mult)
            nc.vector.scalar_tensor_tensor(out=mdif[:, ts], in0=mdif[:, ts], scalar=0.25, in1=mdif[:, ts],
                                           op0=ALU.mult, op1=ALU.mult).then_inc(s["ln_step"], 1)
            dve.wait_ge(s["ln_step"], n * 3 + 2)
            nc.vector.scalar_tensor_tensor(out=vsum[:, ts], in0=vsum[:, ts], scalar=1.0 / H, in1=mdif[:, ts],
                                           op0=ALU.mult, op1=ALU.add).then_inc(s["ln_step"], 1)
            dve.wait_ge(s["ln_step"], n * 3 + 3)
            nc.vector.tensor_scalar(var[:, ts], vsum[:, ts], EPS, None, ALU.add).then_inc(s["var_ready"], 1)

        def normalise(dst, t):
            return nc.vector.tensor_scalar(dst, x_sb[:, t, :], mean[:, bass.ds(t, 1)], rstd[:, bass.ds(t, 1)],
                                           ALU.subtract, ALU.mult)

        def flat(a):
            return a[:, :, :].rearrange("p a b -> p (a b)")

        def over_e(v):
            return v[:, :].unsqueeze(2).broadcast_to([P, NT, E])

        def ffn_vector(dve, f):
            s = ffn[f]
            per = NT // LOADS

            def moments(c):
                if f == 0:
                    dve.wait_ge(x_loaded[c], 16)
                    with dve.Fori(c * per // RING, (c + 1) * per // RING) as q:
                        for r in range(RING):
                            row_stats(q * RING + r).then_inc(s["stats_done"], 1)
                    dve.wait_ge(s["stats_done"], (c + 1) * per)
                layernorm_moments(dve, s, slice(c * per, (c + 1) * per), c)

            def normalised(k):
                later(dve, s["xn_transposed"], k, RING, -RING)
                later(dve, s["xn_stored"][k % 2], k // 2, 16, 0)
                for r in range(RING):
                    normalise(rows[:, k % 2, r, :], k * RING + r).then_inc(s["xn_ready"], 1)

            moments(0)
            for c in range(LOADS):
                if c + 1 < LOADS:
                    moments(c + 1)
                dve.wait_ge(s["rstd_ready"], c + 1)
                for k in range(c * per // RING, (c + 1) * per // RING):
                    normalised(k)

            for i in range(2):
                dve.wait_ge(s["xn_stored"][i], 16 * (NT // RING // 2))
            dve.wait_ge(s["prob_ready"], 1)
            src = prob
            for j in range(TOPK):
                link(dve, nc.vector.tensor_reduce(top[j][:, :], src[:, :, :], AX.X, ALU.max))
                link(dve, nc.vector.tensor_tensor(eq[:, :, :], src[:, :, :], over_e(top[j]), ALU.is_equal))
                link(dve, nc.vector.tensor_tensor(cand[:, :, :], eq[:, :, :],
                                                  rev[:, :].unsqueeze(1).broadcast_to([P, NT, E]), ALU.mult))
                link(dve, nc.vector.tensor_reduce(first[:, :], cand[:, :, :], AX.X, ALU.max))
                link(dve, nc.vector.tensor_tensor(pick[j][:, :, :], cand[:, :, :], over_e(first), ALU.is_equal))
                if j == 0:
                    link(dve, nc.vector.scalar_tensor_tensor(out=flat(rest), in0=flat(pick[0]), scalar=-2.0, in1=flat(prob),
                                                             op0=ALU.mult, op1=ALU.add))
                    src = rest
            nc.vector.tensor_tensor(picks[:, :, :], pick[0][:, :, :], pick[1][:, :, :], ALU.add).then_inc(s["picks_ready"], 1)
            link(dve, nc.vector.tensor_tensor(wsum[:, :], top[0][:, :], top[1][:, :], ALU.add))
            link(dve, nc.vector.reciprocal(wrec[:, :], wsum[:, :]))
            for j in range(TOPK):
                nc.vector.scalar_tensor_tensor(out=weight[:, :, j], in0=top[j][:, :], scalar=0.5, in1=wrec[:, :],
                                               op0=ALU.mult, op1=ALU.mult)
            dve.wait_ge(s["counts_done"], 1)
            link(dve, nc.vector.tensor_copy(tot[:, :, :], bank[4][:, :].rearrange("p (t e) -> p e t", e=E)))
            link(dve, nc.vector.tensor_tensor_scan(flat(cum), flat(seg), flat(tot), 0.0, ALU.mult, ALU.add))
            link(dve, nc.vector.tensor_tensor(more[:, :, :], cum[:, :, NT - 1:NT].broadcast_to([P, E, NT]),
                                              thr[:, :].unsqueeze(1).broadcast_to([P, E, NT]), ALU.is_gt))
            link(dve, nc.vector.tensor_reduce(ntile[:, :], more[:, :, :], AX.X, ALU.add))
            link(dve, nc.vector.tensor_tensor_scan(end[:, :], one_e[:, :], ntile[:, :], 0.0, ALU.mult, ALU.add))
            nc.vector.tensor_scalar(past[:, :], end[0:NE_T, :], place[0:NE_T, :], None, ALU.is_le)
            link(dve, nc.vector.tensor_tensor(begin[:, :], end[:, :], ntile[:, :], ALU.subtract))
            nc.vector.tensor_reduce(passed[:, :], past[:, :], AX.X, ALU.add).then_inc(s["passed_ready"], 1)
            link(dve, nc.vector.tensor_tensor(slot_e[:, :, :], cum[:, :, :], tot[:, :, :], ALU.subtract))
            link(dve, nc.vector.tensor_scalar(begin[:, :], begin[:, :], float(P), None, ALU.mult))
            link(dve, nc.vector.tensor_tensor(slot_e[:, :, :], slot_e[:, :, :],
                                              begin[:, :].unsqueeze(2).broadcast_to([P, E, NT]), ALU.add))
            link(dve, nc.vector.tensor_tensor(slot_t[:, :, :], bank[3][:, :].rearrange("p (t e) -> p t e", e=E),
                                              slot_e[:, :, :].rearrange("p e t -> p t e"), ALU.add))
            for j in range(TOPK):
                link(dve, nc.vector.tensor_tensor(cand[:, :, :], slot_t[:, :, :], pick[j][:, :, :], ALU.mult))
                link(dve, nc.vector.tensor_reduce(slot_f[:, :, j], cand[:, :, :], AX.X, ALU.add))
            link(dve, nc.vector.tensor_copy(slot[:, :, :], slot_f[:, :, :]))

            nc.vector.tensor_scalar(part_u[:, :, :], slot[:, :, :], P - 1, None, ALU.bitwise_and)
            link(dve, nc.vector.tensor_scalar(tile_u[:, :, :], slot[:, :, :], P.bit_length() - 1, None, ALU.logical_shift_right))
            nc.vector.tensor_copy(part_of[:, :, :], part_u[:, :, :])
            link(dve, nc.vector.tensor_copy(tile_of[:, :, :], tile_u[:, :, :]))

            dve.wait_ge(halves_ready, 2)

            def one_hots(k):
                for r in range(PLACES):
                    t, j = k * (PLACES // TOPK) + r // TOPK, r % TOPK
                    later(dve, s["source_done"], k, PLACES, r - PLACES + 1)
                    if j == 0:
                        nc.vector.tensor_scalar(is_part[:, r, :], lane_h[:, :], part_of[:, t, j:j + 1], None, ALU.is_equal)
                    nc.vector.tensor_scalar(is_tile[:, r, :], tile_h[:, :], tile_of[:, t, j:j + 1], token[:, bass.ds(t, 1)],
                                            ALU.is_equal, ALU.mult).then_inc(s["onehot_ready"], 1)

            nc.vector.tensor_scalar(minus_part[:, :], part_of[:, :, 1], -1.0, None, ALU.mult).then_inc(s["minus_part_ready"], 1)
            one_hots(0)
            dve.wait_ge(s["passed_transposed"], 1)
            nc.vector.tensor_scalar(eid[:, :], bank[6][0:1, 0:NE_T], float(E - 1), None, ALU.min).then_inc(s["eid_ready"], 1)
            with dve.Fori(1, NT * TOPK // PLACES) as k:
                one_hots(k)
            dve.wait_ge(s["source_done"], NT * TOPK)
            nc.vector.tensor_scalar(source[:, :], bank[5][:, 0:NE_T], float(NT * P // 2), None, ALU.add)\
                .then_inc(s["source_ready"], 1)

            def gated(u, j):
                dve.wait_ge(s["silu_ready"], j + 1)
                nc.vector.tensor_tensor(hid[:, u, :], bank[2 + u][:, I:2 * I], silu[:, u, :], ALU.mult).then_inc(s["hid_ready"], 1)

            def evac_hid(u, j):
                dve.wait_ge(s["hid_transposed"], j + 1)
                nc.vector.tensor_copy(hidT[:, u, :], bank[4 + u][:, 0:P]).then_inc(s["hidT_ready"], 1)

            def evac_out(r, j, k):
                dve.wait_ge(s["down_done"], j + 1)
                later(dve, s["ye_stored"][r], k, 16, 0)
                nc.vector.tensor_copy(ye[:, r, :], bank[6 + r % 2][:, 0:H]).then_inc(s["ye_ready"], 1)

            def expert_round(k, rs):
                for r in rs:
                    j = k * RING + r
                    if exists(j - 1):
                        evac_hid((r - 1) % 2, j - 1)
                    if exists(j):
                        gated(r % 2, j)
                    if exists(j - 2):
                        evac_out((r - 2) % RING, j - 2, k - 1 if r < 2 else k)

            expert_round(0, range(RING))
            expert_round(1, range(RING))
            with dve.Fori(2, NK - 1) as k:
                expert_round(k, range(RING))
            expert_round(NK - 1, range(RING + 2))

            if f < NF - 1:
                return
            def fetch(r, t):
                nc.vector.tensor_copy(idx[r][0][:, :], slot[:, t, 0:1])
                nc.vector.tensor_copy(idx[r][1][:, :], slot[:, t, 1:2]).then_inc(s["idx_ready"], 1)

            def combine(r, t, k):
                dve.wait_ge(s["gathered"][r], (k + 1) * (16 * TOPK))
                nc.vector.scalar_tensor_tensor(out=mix[:, r % 2, :], in0=got[r][0], scalar=weight[:, t, 0:1],
                                               in1=x_sb[:, t, :], op0=ALU.mult, op1=ALU.add).then_inc(s["mix_ready"], 1)
                dve.wait_ge(s["mix_ready"], t + 1)
                nc.vector.scalar_tensor_tensor(out=x_sb[:, t, :], in0=got[r][1], scalar=weight[:, t, 1:2],
                                               in1=mix[:, r % 2, :], op0=ALU.mult, op1=ALU.add).then_inc(s["x_done"], 1)
                dve.wait_ge(s["x_done"], t + 1)

            for r in range(RING):
                dve.wait_ge(s["xe_loaded"][r], 16 * NK)
                fetch(r, r)
            with dve.Fori(0, NT // RING - 1) as k:
                for r in range(RING):
                    combine(r, k * RING + r, k)
                    fetch(r, k * RING + RING + r)
            for r in range(RING):
                combine(r, NT - RING + r, NT // RING - 1)

        @block.vector
        def _(dve):
            dve.wait_ge(gwT_made, 1)
            dve.wait_ge(consts, 12)
            nc.vector.memset(gwT[:, :, E:EW], 0.0)
            nc.vector.tensor_copy(lane_h[:, :], lane[:, :]).then_inc(halves_ready, 1)
            nc.vector.tensor_copy(tile_h[:, :], tile_no[:, :]).then_inc(halves_ready, 1)
            nc.vector.tensor_copy(gwT[:, :, 0:E], bank[7][:, 0:HC * E].rearrange("p (c e) -> p c e", e=E)).then_inc(gwT_ready, 1)
            dve.wait_ge(consts, 12)
            for n, st in enumerate(stages):
                if st == "ffn":
                    ffn_vector(dve, stages[:n].count("ffn"))
                else:
                    attn_vector(dve)


_INS = ["L0_attn_x", "L0_attn_w_qkv", "L0_attn_w_out", "L0_ffn_gate_w", "L0_ffn_gate_up_proj", "L0_ffn_down_proj"]


def kernel(**inputs):
    import numpy as _np
    import concourse.bacc as _bacc
    from concourse.bass_utils import run_bass_kernel_spmd as _run

    nc = _bacc.Bacc("TRN2", target_bir_lowering=False, num_devices=1)
    arrays, args = {}, []
    for name in _INS:
        a = _np.ascontiguousarray(inputs[name])
        arrays[f"in_{name}_dram"] = a
        args.append(nc.dram_tensor(f"in_{name}_dram", a.shape, mybir.dt.from_np(a.dtype), kind="ExternalInput").ap())
    shape = arrays["in_L0_attn_x_dram"].shape
    args.append(nc.dram_tensor("out_0_dram", shape, F32, kind="ExternalOutput").ap())
    macaron_block(nc, *args)
    r = _run(nc, [arrays], core_ids=[0])
    return r.results[0]["out_0_dram"]
```
